# Optimizing a Trainium2 kernel written in Bass

```python
import numpy as np
import jax
import jax.numpy as jnp

def _softmax(x, axis=-1):
    return jax.nn.softmax(x, axis=axis)

def _gelu(x):
    return jax.nn.gelu(x, approximate=True)

def _silu(x):
    return jax.nn.silu(x)

def _sigmoid(x):
    return jax.nn.sigmoid(x)

def _layernorm(x, axis=-1, eps=1e-05):
    m = jnp.mean(x, axis=axis, keepdims=True)
    v = jnp.var(x, axis=axis, keepdims=True)
    return (x - m) / jnp.sqrt(v + eps)

def _scatter_add(tgt, idx, src, axis=0):
    return tgt.at[idx].add(src)

def _segment_sum(src, seg, n):
    return jax.ops.segment_sum(src, seg, n)
kernel_name = 'mk_decoder_preln_d1_seqx_r8_6d1da4'

def setup_inputs(seed: int=0):
    np.random.seed(seed)
    _w = jnp.asarray

    def _rec_inputs():
        import jax
        import jax.numpy as jnp
        _rk = jax.random.key(seed)
        x = -0.0002928 + 1 * jax.random.normal(jax.random.fold_in(_rk, 1), (4, 512, 128), jnp.float32)
        _lenS = 512 - jax.random.randint(jax.random.fold_in(_rk, 7), (4,), 0, max(1, 512 // 4) + 1, jnp.int32)
        _lenS2 = 77 - jax.random.randint(jax.random.fold_in(_rk, 8), (4,), 0, max(1, 77 // 4) + 1, jnp.int32)
        _ctx_1024P = jax.random.normal(jax.random.fold_in(_rk, 11), (4, 16, 128), jnp.float32)
        _ctx_1024c = jax.random.dirichlet(jax.random.fold_in(_rk, 511), 0.3 * jnp.ones((16,), jnp.float32), (4, 77))
        _ctx_1024t = jnp.einsum('bsk,bkd->bsd', _ctx_1024c, _ctx_1024P)
        _ctx_1024t = _ctx_1024t * jax.lax.rsqrt(jnp.mean(jnp.square(_ctx_1024t)) + 1e-12) * 0.953939
        ctx_1024 = -1.39393e-06 + 0.999914 * (_ctx_1024t + 0.3 * jax.random.normal(jax.random.fold_in(_rk, 611), (4, 77, 128), jnp.float32))
        _validS = jnp.arange(512)[None, :] < _lenS[:, None]
        _validS2 = jnp.arange(77)[None, :] < _lenS2[:, None]
        _causal = jnp.tril(jnp.ones((512, 512), dtype=bool))
        mask_BxS2_ik0 = jnp.where(jnp.broadcast_to(_validS2[:, :], (4, 77)), 0, 1).astype(jnp.int32)
        return (x, ctx_1024, mask_BxS2_ik0)
    x, ctx_1024, mask_BxS2_ik0 = _rec_inputs()

    def _L0_attn_setup():
        import jax, jax.numpy as jnp
        import numpy as np
        import math
        D_MODEL = 128
        N_HEADS = 16
        DECAY_SCALE = 0.25

        def power_law_mask(n, decay_scale):
            i = jnp.arange(n)[:, None]
            j = jnp.arange(n)[None, :]
            delta = (i - j).astype(jnp.float32)
            decay = jnp.where(delta > 0, -decay_scale * jnp.log(jnp.maximum(delta, 1.0)), 0.0)
            return jnp.where(j > i, -jnp.inf, decay)
        key = jax.random.key(seed)
        ks = jax.random.split(key, 9)
        B, N, D = (2, 256, D_MODEL)
        s = 1.0 / math.sqrt(D)
        return {'x': jax.random.normal(ks[0], (B, N, D), dtype=jnp.float32), 'Wq': jax.random.normal(ks[1], (D, D), dtype=jnp.float32) * s, 'bq': jnp.zeros((D,), dtype=jnp.float32), 'Wk': jax.random.normal(ks[2], (D, D), dtype=jnp.float32) * s, 'bk': jnp.zeros((D,), dtype=jnp.float32), 'Wv': jax.random.normal(ks[3], (D, D), dtype=jnp.float32) * s, 'bv': jnp.zeros((D,), dtype=jnp.float32), 'Wo': jax.random.normal(ks[4], (D, D), dtype=jnp.float32) * s, 'bo': jnp.zeros((D,), dtype=jnp.float32)}
    _L0_attn_all = _L0_attn_setup()
    _L0_attn_in = {k: v for k, v in _L0_attn_all.items() if k in ('Wq', 'bq', 'Wk', 'bk', 'Wv', 'bv', 'Wo', 'bo')}
    del _L0_attn_all

    def _L0_xattn_setup():
        import jax, jax.numpy as jnp
        import numpy as np
        B, SQ, SKV, D, H = (2, 256, 256, 128, 16)
        W = D // H

        def _heads(x):
            b, s, _ = x.shape
            return x.reshape(b, s, H, W).transpose(0, 2, 1, 3)
        key = jax.random.key(seed)
        ks = jax.random.split(key, 10)
        s = 1.0 / np.sqrt(D)
        return {'x_q': jax.random.normal(ks[0], (B, SQ, D), jnp.float32), 'x_k': jax.random.normal(ks[1], (B, SKV, D), jnp.float32), 'x_v': jax.random.normal(ks[2], (B, SKV, D), jnp.float32), 'mask': jax.random.randint(ks[3], (B, SKV), 0, 2, jnp.int32), 'Wq': jax.random.normal(ks[4], (D, D), jnp.float32) * s, 'bq': jnp.zeros((D,), jnp.float32), 'Wk': jax.random.normal(ks[5], (D, D), jnp.float32) * s, 'bk': jnp.zeros((D,), jnp.float32), 'Wv': jax.random.normal(ks[6], (D, D), jnp.float32) * s, 'bv': jnp.zeros((D,), jnp.float32)}
    _L0_xattn_all = _L0_xattn_setup()
    _L0_xattn_in = {k: v for k, v in _L0_xattn_all.items() if k in ('Wq', 'bq', 'Wk', 'bk', 'Wv', 'bv')}
    del _L0_xattn_all

    def _L0_ffn_setup():
        import jax, jax.numpy as jnp
        import numpy as np
        H = 128
        I = 64
        E = 8
        TOP_K = 2
        N_SHARED = 2
        SHARED_I = I * N_SHARED
        SCALE = 2.5
        NORM_TOPK = True
        B, S = (2, 128)

        def _swiglu(x, wg, wu, wd):
            g = x @ wg.T
            u = x @ wu.T
            return jax.nn.silu(g) * u @ wd.T
        key = jax.random.key(seed)
        ks = jax.random.split(key, 8)
        std = 0.02
        return {'hidden_states': jax.random.normal(ks[0], (B, S, H), jnp.float32), 'gate_weight': jax.random.normal(ks[1], (E, H), jnp.float32) * std, 'w_gate': jax.random.normal(ks[2], (E, I, H), jnp.float32) * std, 'w_up': jax.random.normal(ks[3], (E, I, H), jnp.float32) * std, 'w_down': jax.random.normal(ks[4], (E, H, I), jnp.float32) * std, 'ws_gate': jax.random.normal(ks[5], (SHARED_I, H), jnp.float32) * std, 'ws_up': jax.random.normal(ks[6], (SHARED_I, H), jnp.float32) * std, 'ws_down': jax.random.normal(ks[7], (H, SHARED_I), jnp.float32) * std}
    _L0_ffn_all = _L0_ffn_setup()
    _L0_ffn_in = {k: v for k, v in _L0_ffn_all.items() if k in ('gate_weight', 'w_gate', 'w_up', 'w_down', 'ws_gate', 'ws_up', 'ws_down')}
    del _L0_ffn_all
    return {'x': x, 'ctx_1024': ctx_1024, 'mask_BxS2_ik0': mask_BxS2_ik0, 'L0_attn_Wq': _L0_attn_in['Wq'], 'L0_attn_bq': _L0_attn_in['bq'], 'L0_attn_Wk': _L0_attn_in['Wk'], 'L0_attn_bk': _L0_attn_in['bk'], 'L0_attn_Wv': _L0_attn_in['Wv'], 'L0_attn_bv': _L0_attn_in['bv'], 'L0_attn_Wo': _L0_attn_in['Wo'], 'L0_attn_bo': _L0_attn_in['bo'], 'L0_xattn_Wq': _L0_xattn_in['Wq'], 'L0_xattn_bq': _L0_xattn_in['bq'], 'L0_xattn_Wk': _L0_xattn_in['Wk'], 'L0_xattn_bk': _L0_xattn_in['bk'], 'L0_xattn_Wv': _L0_xattn_in['Wv'], 'L0_xattn_bv': _L0_xattn_in['bv'], 'L0_ffn_gate_weight': _L0_ffn_in['gate_weight'], 'L0_ffn_w_gate': _L0_ffn_in['w_gate'], 'L0_ffn_w_up': _L0_ffn_in['w_up'], 'L0_ffn_w_down': _L0_ffn_in['w_down'], 'L0_ffn_ws_gate': _L0_ffn_in['ws_gate'], 'L0_ffn_ws_up': _L0_ffn_in['ws_up'], 'L0_ffn_ws_down': _L0_ffn_in['ws_down']}

def reference(x, ctx_1024, mask_BxS2_ik0, L0_attn_Wq, L0_attn_bq, L0_attn_Wk, L0_attn_bk, L0_attn_Wv, L0_attn_bv, L0_attn_Wo, L0_attn_bo, L0_xattn_Wq, L0_xattn_bq, L0_xattn_Wk, L0_xattn_bk, L0_xattn_Wv, L0_xattn_bv, L0_ffn_gate_weight, L0_ffn_w_gate, L0_ffn_w_up, L0_ffn_w_down, L0_ffn_ws_gate, L0_ffn_ws_up, L0_ffn_ws_down):
    import jax
    import jax.numpy as jnp

    def _L0_attn_ref(x, Wq, bq, Wk, bk, Wv, bv, Wo, bo):
        import jax, jax.numpy as jnp
        import numpy as np
        import math
        D_MODEL = 128
        N_HEADS = 16
        DECAY_SCALE = 0.25

        def power_law_mask(n, decay_scale):
            i = jnp.arange(n)[:, None]
            j = jnp.arange(n)[None, :]
            delta = (i - j).astype(jnp.float32)
            decay = jnp.where(delta > 0, -decay_scale * jnp.log(jnp.maximum(delta, 1.0)), 0.0)
            return jnp.where(j > i, -jnp.inf, decay)
        B, N, D = x.shape
        H = N_HEADS
        dk = D // H

        def proj(W, b):
            return (x @ W + b).reshape(B, N, H, dk).transpose(0, 2, 1, 3)
        Q, K, V = (proj(Wq, bq), proj(Wk, bk), proj(Wv, bv))
        scores = jnp.einsum('bhnd,bhmd->bhnm', Q, K) / jnp.sqrt(jnp.float32(dk))
        scores = scores + power_law_mask(N, DECAY_SCALE)[None, None]
        attn = jax.nn.softmax(scores, axis=-1)
        out = jnp.einsum('bhnm,bhmd->bhnd', attn, V)
        out = out.transpose(0, 2, 1, 3).reshape(B, N, D)
        return out @ Wo + bo

    def _L0_xattn_ref(x_q, x_k, x_v, mask, Wq, bq, Wk, bk, Wv, bv):
        import jax, jax.numpy as jnp
        import numpy as np
        B, SQ, SKV, D, H = (2, 256, 256, 128, 16)
        W = D // H

        def _heads(x):
            b, s, _ = x.shape
            return x.reshape(b, s, H, W).transpose(0, 2, 1, 3)
        q = _heads(x_q @ Wq.T + bq)
        k = _heads(x_k @ Wk.T + bk)
        v = _heads(x_v @ Wv.T + bv)
        scores = jnp.einsum('bhqw,bhkw->bhqk', q, k) / np.sqrt(W).astype(np.float32)
        m = mask[:, None, None, :].astype(scores.dtype)
        scores = scores - 10000.0 * (1.0 - m)
        p = jax.nn.softmax(scores, axis=-1)
        h = jnp.einsum('bhqk,bhkw->bhqw', p, v)
        return h.transpose(0, 2, 1, 3).reshape(x_q.shape[0], x_q.shape[1], D)

    def _L0_ffn_ref(hidden_states, gate_weight, w_gate, w_up, w_down, ws_gate, ws_up, ws_down):
        import jax, jax.numpy as jnp
        import numpy as np
        H = 128
        I = 64
        E = 8
        TOP_K = 2
        N_SHARED = 2
        SHARED_I = I * N_SHARED
        SCALE = 2.5
        NORM_TOPK = True
        B, S = (2, 128)

        def _swiglu(x, wg, wu, wd):
            g = x @ wg.T
            u = x @ wu.T
            return jax.nn.silu(g) * u @ wd.T
        b, s, h = hidden_states.shape
        x = hidden_states.reshape(-1, h)
        shared_out = _swiglu(x, ws_gate, ws_up, ws_down)
        logits = x.astype(jnp.float32) @ gate_weight.astype(jnp.float32).T
        scores = jax.nn.sigmoid(logits)
        topk_w, topk_idx = jax.lax.top_k(scores, TOP_K)
        if TOP_K > 1 and NORM_TOPK:
            topk_w = topk_w / (topk_w.sum(-1, keepdims=True) + 1e-20)
        topk_w = topk_w * SCALE
        onehot = jax.nn.one_hot(topk_idx, E, dtype=topk_w.dtype)
        combine = jnp.einsum('tk,tke->te', topk_w, onehot)
        g = jnp.einsum('th,eih->tei', x, w_gate)
        u = jnp.einsum('th,eih->tei', x, w_up)
        hmid = jax.nn.silu(g) * u
        y = jnp.einsum('tei,ehi->teh', hmid, w_down)
        routed_out = jnp.einsum('te,teh->th', combine, y)
        out = (routed_out + shared_out).reshape(b, s, h)
        return out
    x = x + _L0_attn_ref(_layernorm(x, axis=-1), L0_attn_Wq, L0_attn_bq, L0_attn_Wk, L0_attn_bk, L0_attn_Wv, L0_attn_bv, L0_attn_Wo, L0_attn_bo)
    x = x + _L0_xattn_ref(_layernorm(x, axis=-1), ctx_1024, ctx_1024, mask_BxS2_ik0, L0_xattn_Wq, L0_xattn_bq, L0_xattn_Wk, L0_xattn_bk, L0_xattn_Wv, L0_xattn_bv)
    x = x + _L0_ffn_ref(_layernorm(x, axis=-1), L0_ffn_gate_weight, L0_ffn_w_gate, L0_ffn_w_up, L0_ffn_w_down, L0_ffn_ws_gate, L0_ffn_ws_up, L0_ffn_ws_down)
    return x

_drawn_inputs = setup_inputs


def setup_inputs(seed=0):
    import zlib

    import numpy as np

    out = dict(_drawn_inputs(seed))
    spreads = {'L0_attn_bq': (0.0, 0.591),
     'L0_attn_bk': (0.0, 0.8),
     'L0_attn_bv': (0.0, 0.1),
     'L0_attn_bo': (0.0, 0.1),
     'L0_xattn_bq': (0.0, 0.1),
     'L0_xattn_bk': (0.0, 0.8),
     'L0_xattn_bv': (0.0, 0.1)}
    factors = {'L0_ffn_gate_weight': 8.0,
     'L0_ffn_w_gate': 8.0,
     'L0_ffn_w_up': 8.0,
     'L0_ffn_w_down': 8.0,
     'L0_ffn_ws_gate': 8.0,
     'L0_ffn_ws_up': 8.0,
     'L0_ffn_ws_down': 8.0}
    for name, (base, spread) in spreads.items():
        noise = np.random.default_rng([zlib.crc32(name.encode()), seed]).standard_normal(out[name].shape)
        drawn = base * np.exp(spread * noise) if base else spread * noise
        out[name] = jnp.asarray(drawn.astype(out[name].dtype))
    for name, factor in factors.items():
        out[name] = (out[name] * factor).astype(out[name].dtype)
    return out
```

```python
import struct
from contextlib import ExitStack

import concourse.bass as bass
from concourse import mybir

ALU = mybir.AluOpType
ACT = mybir.ActivationFunctionType
AX_X = mybir.AxisListType.X
F32 = mybir.dt.float32
BF16 = mybir.dt.bfloat16
I32 = mybir.dt.int32
U32 = mybir.dt.uint32

P = 128
B = 4
N = 512
NT = N // P
H = 16
DK = P // H
NK = 77
E = 8
FC = 5
NPART = 3
QK = NPART * NPART * DK
ROWX = 96
KM = 96
KS = ROWX + NPART
KMX = ROWX + NPART
KSX = ROWX + 2 * NPART
SCALE = float(DK) ** -0.5
EPS = 1e-5
ROUTE = 2.5
TWO_ONES = struct.unpack("f", struct.pack("I", 0x3F803F80))[0]
START = 1
FAR = -1e30

MAX_TILES = [(qt, h, n) for qt in range(NT) for n in [4 // (qt + 1) if qt < 2 else 1] for h in range(0, H, n)]
XMAX_TILES = [(qt, h, n) for qt in range(NT) for h, n in ((0, 6), (6, 5), (11, 5))]
PIECES = ([[(g, 0, 0)] for g in range(4)]
          + [[(g, 1, 0), (g, 3, 384)] for g in range(4)]
          + [[(0, 2, 0), (1, 2, 256)], [(2, 2, 0), (3, 2, 256)]])
SETS = [(0, 4), (4, 8), (8, 10)]
GROUPS = [(half, e) for half in range(2) for e in range(2)]
TPG = len(PIECES)
TILES = TPG * len(GROUPS)
POOL_TILES = (0, 5, 9)


def head(half, e, g):
    return 8 * half + 2 * g + e


def on_pool(t):
    return t % TPG in POOL_TILES


def applied_before(t, pool):
    return sum(on_pool(x) == pool for x in range(t + 1))


POOL_N, DVE_N = applied_before(TILES - 1, True), applied_before(TILES - 1, False)


def decoder_layer(nc, x, ctx_in, mask, wq, wk, wv, wo, wxq, wxk, wxv, bias_cols, bias_rows,
                  wg, wu, wd, gate, ident, diag, decay, sel, iota, out):
    x_v = x.rearrange("b (t p) d -> b p t d", p=P)
    out_v = out.rearrange("b (t p) d -> b p t d", p=P)

    ctx = ExitStack()
    with ctx:
        def sb(name, shape, dt=F32):
            return ctx.enter_context(nc.sbuf_tensor(name, shape, dt))

        def sem(name):
            s = ctx.enter_context(nc.semaphore(name))
            counted.append(s)
            return s

        counted = []

        q_scr = nc.dram_tensor("q_scr", (NPART, P, N), BF16, kind="Internal").ap()
        k_scr = nc.dram_tensor("k_scr", (NPART, P, N), BF16, kind="Internal").ap()
        qx_scr = nc.dram_tensor("qx_scr", (NPART, P, N), BF16, kind="Internal").ap()
        mask_scr = nc.dram_tensor("mask_scr", (NPART, B, P), BF16, kind="Internal").ap()
        mx_scr = nc.dram_tensor("mx_scr", (NPART * H, N), BF16, kind="Internal").ap()
        mxx_scr = nc.dram_tensor("mxx_scr", (NPART * H, N), BF16, kind="Internal").ap()
        kx_scr = nc.dram_tensor("kx_scr", (NPART, P, NK), BF16, kind="Internal").ap()

        w_sb = sb("w_sb", [P, 7, P])
        WQ, WK, WV, WO, WXQ, WXK, WXV = range(7)
        bcol = sb("bcol", [P, 4])
        brow = sb("brow", [P, 3, P])
        wg_sb = sb("wg_sb", [P, FC * P])
        wu_sb = sb("wu_sb", [P, FC * P])
        wd_sb = sb("wd_sb", [P, FC, P])
        gate_sb = sb("gate_sb", [P, E])
        id_f = sb("id_f", [P, P])
        id_b = sb("id_b", [P, P], BF16)
        diag_f = sb("diag_f", [P, P])
        diag_b = sb("diag_b", [P, P], BF16)
        dec = sb("dec", [P, 3, N])
        sel_f = sb("sel_f", [P, 4, P])
        sel_b = sb("sel_b", [P, 4, P], BF16)
        iota_sb = sb("iota_sb", [P, E])
        spare = sb("spare", [P, 4])
        half_pow = sb("half_pow", [P, NT])
        eps_sb = sb("eps_sb", [P, NT])
        mask_i = sb("mask_i", [B, NK], I32)
        mask_s = sb("mask_s", [B, 2, P])
        mask_b = sb("mask_b", [B, NPART, P], BF16)

        xin = sb("xin", [P, NT, P])
        xb = sb("xb", [P, NT, P])
        stats = sb("stats", [P, NT, 6])
        mv = sb("mv", [P, NT, 2])
        ve = sb("ve", [P, NT])
        rstd = sb("rstd", [P, NT])
        xn = sb("xn", [P, NT, P])
        xnT = sb("xnT", [P, N])
        qk_f = sb("qk_f", [P, 2, N])
        qk_r = sb("qk_r", [P, 2, N])
        q_part = sb("q_part", [P, NPART, N], BF16)
        k_part = sb("k_part", [P, NPART, N], BF16)
        Qs = sb("Qs", [P, H, N], BF16)
        Ks = sb("Ks", [P, H, N], BF16)
        Vs = sb("Vs", [P, NT, H, 32])
        mx = sb("mx", [P, NT, H])
        mx_r = sb("mx_r", [P, NT, H])
        mx_part = sb("mx_part", [P, NT, P // H, H], BF16)
        mxT = sb("mxT", [NPART * H, N], BF16)
        Ps = sb("Ps", [P, TPG, N])
        Nh = sb("Nh", [P, 2, N])
        den = sb("den", [P, NT * 4, 2])
        at = sb("at", [P, NT, P])
        atT = sb("atT", [P, N])
        x1 = sb("x1", [P, NT, P])

        cin = sb("cin", [NK, P])
        cT = sb("cT", [P, NK])
        kx_f = sb("kx_f", [P, NK])
        kx_r = sb("kx_r", [P, NK])
        kx_part = sb("kx_part", [P, NPART, NK], BF16)
        Kx = sb("Kx", [P, H, P], BF16)
        Vx = sb("Vx", [P, H, 32])
        statsx = sb("statsx", [P, NT, 6])
        mvx = sb("mvx", [P, NT, 2])
        vex = sb("vex", [P, NT])
        rstdx = sb("rstdx", [P, NT])
        xn2 = sb("xn2", [P, NT, P])
        xn2T = sb("xn2T", [P, N])
        qx_f = sb("qx_f", [P, N])
        qx_r = sb("qx_r", [P, N])
        qx_part = sb("qx_part", [P, NPART, N], BF16)
        Qx = sb("Qx", [P, H, N], BF16)
        mxx = sb("mxx", [P, NT, H])
        mxx_r = sb("mxx_r", [P, NT, H])
        mxx_part = sb("mxx_part", [P, NT, P // H, H], BF16)
        mxxT = sb("mxxT", [NPART * H, N], BF16)
        Px = sb("Px", [P, 8, N])
        Nx = sb("Nx", [P, 2, N])
        denx = sb("denx", [P, NT * 4, 2])
        atx = sb("atx", [P, NT, P])
        x2 = sb("x2", [P, NT, P])
        eg = sb("eg", [P, NT, E])
        sg = sb("sg", [P, NT, E])
        top = sb("top", [P, NT, 8])
        topi = sb("topi", [P, NT, 8], U32)
        topf = sb("topf", [P, NT, 2])
        wsum = sb("wsum", [P, NT, 1])
        topw = sb("topw", [P, NT, 2])
        comb = sb("comb", [P, 2, NT, E])
        comb_f = sb("comb_f", [P, NT, E])
        comb_r = sb("comb_r", [P, NT, E])
        comb_part = sb("comb_part", [P, NT, P // E, E], BF16)
        combT = sb("combT", [P, N], BF16)
        th = sb("th", [P, 2, N])
        ga = sb("ga", [P, 2, N])
        hm = sb("hm", [P, FC, N])
        yo = sb("yo", [P, NT, P])

        bank = [ctx.enter_context(nc.psum_tensor(f"bank{i}", [P, N], F32)) for i in range(8)]
        sc_bank = bank[0:2]
        mx_bank = bank[2:4]
        s_bank = bank[4]
        c_bank = bank[5:7]
        x_bank = bank[7]

        w_in = sem("w_in")
        mask_in = sem("mask_in")
        set_up = sem("set_up")
        mask_ready = sem("mask_ready")
        mask_out = sem("mask_out")
        preset = sem("preset")

        counted.clear()
        x_in = sem("x_in")
        s_ln = sem("s_ln")
        s_rstd = sem("s_rstd")
        s_tr = sem("s_tr")
        s_proj = sem("s_proj")
        s_split = sem("s_split")
        scr_out = sem("scr_out")
        stack_in = sem("stack_in")
        max_ready = sem("max_ready")
        mb_free = [sem("mb_free0"), sem("mb_free1")]
        mx_split = sem("mx_split")
        mx_tr = sem("mx_tr")
        max_row = sem("max_row")
        sc_ready = sem("sc_ready")
        exp_done = sem("exp_done")
        dec_dve = sem("dec_dve")
        dec_pool = sem("dec_pool")
        pv_done = sem("pv_done")
        sb_free = sem("sb_free")
        n_tr = sem("n_tr")
        s_norm = sem("s_norm")

        mask_rows = sem("mask_rows")
        ctx_in_s = sem("ctx_in_s")
        x_ln = sem("x_ln")
        x_rstd = sem("x_rstd")
        c_ready = sem("c_ready")
        c_free = [sem("c_free0"), sem("c_free1")]
        x_split = sem("x_split")
        xscr_out = sem("xscr_out")
        xk_in = sem("xk_in")
        xq_in = sem("xq_in")
        xmx_split = sem("xmx_split")
        xmax_row = sem("xmax_row")
        xpv_done = sem("xpv_done")
        xb_ready = sem("xb_ready")
        xb_free = sem("xb_free")
        x_norm = sem("x_norm")
        g_sig = sem("g_sig")
        g_step = sem("g_step")
        tanh_done = sem("tanh_done")
        gate_done = sem("gate_done")
        down_done = sem("down_done")
        y_ready = sem("y_ready")
        y_out = sem("y_out")

        with nc.Block() as start:
            @start.sync
            def _(sp):
                for s in counted:
                    sp.sem_inc(s, START)

        N_W = 7 + 4 + 3 + 11
        block = ctx.enter_context(nc.Block())

        @block.sync
        def _(sp):
            sp.dma_start(mask_i[:, :], mask).then_inc(mask_in, 16)
            for i, w in enumerate((wq, wk, wv, wo, wxq, wxk, wxv)):
                sp.dma_start(w_sb[:, i, :], w).then_inc(w_in, 16)
            for i in range(4):
                sp.dma_start(bcol[:, i:i + 1], bias_cols[i].rearrange("(d o) -> d o", o=1)).then_inc(w_in, 16)
            for i in range(3):
                sp.dma_start(brow[:, i, :], bias_rows[i].partition_broadcast(P)).then_inc(w_in, 16)
            sp.dma_start(id_f[:, :], ident).then_inc(w_in, 16)
            sp.dma_start(diag_f[:, :], diag).then_inc(w_in, 16)
            sp.dma_start(dec[:, 0, :], decay).then_inc(w_in, 16)
            sp.dma_start(dec[:, 1, 0:384], decay[:, 0:384]).then_inc(w_in, 16)
            sp.dma_start(dec[:, 1, 384:512], decay[:, 0:128]).then_inc(w_in, 16)
            sp.dma_start(dec[:, 2, 0:256], decay[:, 0:256]).then_inc(w_in, 16)
            sp.dma_start(dec[:, 2, 256:512], decay[:, 0:256]).then_inc(w_in, 16)
            sp.dma_start(sel_f[:, :, :], sel).then_inc(w_in, 16)
            sp.dma_start(iota_sb[:, :], iota).then_inc(w_in, 16)
            sp.dma_start(gate_sb[:, :], gate).then_inc(w_in, 16)
            sp.dma_start(wd_sb[:, :, :], wd.rearrange("c f h -> f c h")).then_inc(w_in, 16)
            sp.dma_start(wg_sb[:, :], wg).then_inc(mask_in, 16)
            sp.dma_start(wu_sb[:, :], wu).then_inc(mask_in, 16)

            def load_x(b):
                sp.wait_ge(s_ln, START + 3 * b)
                sp.wait_ge(s_rstd, START + 3 * b)
                sp.dma_start(xin[:, :, :], x_v[b]).then_inc(x_in, 16)

            def s_dmas(b):
                sp.wait_ge(sc_ready, START + TILES * b)
                sp.wait_ge(s_split, START + 6 * b + 6)
                sp.dma_start(q_scr.rearrange("i r t -> r i t"), q_part[:, :, :]).then_inc(scr_out, 16)
                sp.dma_start(k_scr.rearrange("i r t -> r i t"), k_part[:, :, :]).then_inc(scr_out, 16)
                sp.wait_ge(scr_out, START + 32 * b + 32)
                for i in range(NPART):
                    for r in range(NPART):
                        row = DK * (NPART * i + r)
                        sp.dma_start(Qs[row:row + DK, :, :],
                                     q_scr[i].rearrange("(h d) t -> d h t", d=DK)).then_inc(stack_in, 16)
                        sp.dma_start(Ks[row:row + DK, :, :],
                                     k_scr[r].rearrange("(h d) t -> d h t", d=DK)).then_inc(stack_in, 16)

            def s_max_rows(b):
                sp.wait_ge(sb_free, START + 7 * b + 1)
                sp.dma_start(mx_scr, mxT[:, :]).then_inc(max_row, 16)
                sp.wait_ge(max_row, START + 32 * b + 16)
                sp.dma_start(Qs[ROWX:ROWX + NPART, :, :], mx_scr.rearrange("(i h) t -> i h t", h=H)).then_inc(max_row, 16)

            def load_ctx(b):
                sp.wait_ge(c_ready, START + 44 * b)
                sp.dma_start(cin[:, :], ctx_in[b]).then_inc(ctx_in_s, 16)

            def mask_row(b):
                sp.wait_ge(xpv_done, START + 4 * b)
                for i in range(NPART):
                    sp.dma_start(Kx[ROWX + i:ROWX + i + 1, :, :],
                                 mask_scr[i:i + 1, bass.ds(b, 1), :].broadcast_to([1, H, P]))\
                      .then_inc(mask_rows, 16)

            def x_keys(b):
                sp.wait_ge(x_split, START + 6 * b + 3)
                sp.dma_start(kx_scr.rearrange("i r t -> r i t"), kx_part[:, :, :]).then_inc(xscr_out, 16)
                sp.wait_ge(xscr_out, START + 32 * b + 16)
                for i in range(NPART):
                    for r in range(NPART):
                        row = DK * (NPART * i + r)
                        sp.dma_start(Kx[row:row + DK, :, 0:NK],
                                     kx_scr[r].rearrange("(h d) t -> d h t", d=DK)).then_inc(xk_in, 16)

            def x_queries(b):
                sp.wait_ge(x_split, START + 6 * b + 6)
                sp.dma_start(qx_scr.rearrange("i r t -> r i t"), qx_part[:, :, :]).then_inc(xscr_out, 16)
                sp.wait_ge(xscr_out, START + 32 * b + 32)
                for i in range(NPART):
                    for r in range(NPART):
                        row = DK * (NPART * i + r)
                        sp.dma_start(Qx[row:row + DK, :, :],
                                     qx_scr[i].rearrange("(h d) t -> d h t", d=DK)).then_inc(xq_in, 16)

            def x_max_rows(b):
                sp.wait_ge(xb_free, START + 7 * b + 1)
                sp.dma_start(mxx_scr, mxxT[:, :]).then_inc(xmax_row, 16)
                sp.wait_ge(xmax_row, START + 32 * b + 16)
                sp.dma_start(Qx[ROWX + NPART:ROWX + 2 * NPART, :, :], mxx_scr.rearrange("(i h) t -> i h t", h=H))\
                  .then_inc(xmax_row, 16)

            def store_y(b):
                sp.wait_ge(y_ready, START + b + 1)
                sp.dma_start(out_v[b], yo[:, :, :]).then_inc(y_out, 16)

            sp.wait_ge(preset, 1)
            sp.wait_ge(mask_ready, 6)
            sp.dma_start(mask_scr.rearrange("i b k -> b i k"), mask_b[:, :, :]).then_inc(mask_out, 16)
            sp.wait_ge(mask_out, 16)
            with sp.Fori(0, B) as b:
                load_x(b)
                load_ctx(b)
                s_dmas(b)
                s_max_rows(b)
                mask_row(b)
                x_keys(b)
                x_queries(b)
                x_max_rows(b)
                store_y(b)
            sp.wait_ge(y_out, START + 16 * B)

        @block.gpsimd
        def _(pool):
            for stack in (Qs, Ks, Qx, Kx):
                pool.memset(stack[0:ROWX, :, :].bitcast(F32), 0.0)
            pool.memset(Vs[:, :, :, :], 0.0)
            pool.memset(Vx[:, :, :], 0.0)
            pool.memset(combT[:, :], 0.0)
            for part in (mx_part, mxx_part, comb_part):
                pool.memset(part[:, :, :, :], 0.0)
            pool.memset(eps_sb[:, :], EPS)
            pool.memset(half_pow[:, :], -0.5).then_inc(preset, 1)
            pool.wait_ge(preset, 1)
            for e in range(2):
                pool.memset(Vs[:, :, e:H:2, 16 + 8 * e:24 + 8 * e], 1.0)
                pool.memset(Vx[:, e:H:2, 16 + 8 * e:24 + 8 * e], 1.0).then_inc(preset, 1)
            pool.wait_ge(w_in, 16 * N_W)
            pool.wait_ge(preset, 3)

            def s_norm_step(b):
                pool.wait_ge(s_ln, START + 3 * b + 2)
                pool.tensor_tensor(ve[:, :], mv[:, :, 1], eps_sb[:, :], ALU.add).then_inc(s_rstd, 1)
                pool.wait_ge(s_rstd, START + 3 * b + 1)
                pool.tensor_tensor(rstd[:, :], ve[:, :], half_pow[:, :], ALU.pow).then_inc(s_rstd, 1)
                pool.wait_ge(x_in, START + 16 * b + 16)
                pool.wait_ge(sb_free, START + 7 * b)
                pool.tensor_tensor(xb[:, :, :], xin[:, :, :], brow[:, 1:2, :].broadcast_to([P, NT, P]),
                                   ALU.add).then_inc(s_rstd, 1)

            def x_norm_step(b, k):
                pool.wait_ge(x_ln, START + 6 * b + 3 * k + 2)
                pool.tensor_tensor(vex[:, :], mvx[:, :, 1], eps_sb[:, :], ALU.add).then_inc(x_rstd, 1)
                pool.wait_ge(x_rstd, START + 4 * b + 2 * k + 1)
                pool.tensor_tensor(rstdx[:, :], vex[:, :], half_pow[:, :], ALU.pow).then_inc(x_rstd, 1)

            def decay_tiles(b):
                for t in range(TILES):
                    if on_pool(t):
                        kind = 0 if t % TPG < 4 else 1 if t % TPG < 8 else 2
                        pool.wait_ge(exp_done, START + TILES * b + t + 1)
                        pool.tensor_tensor(Ps[:, t % TPG, :], Ps[:, t % TPG, :], dec[:, kind, :],
                                           ALU.mult).then_inc(dec_pool, 1)

            with pool.Fori(0, B) as b:
                s_norm_step(b)
                decay_tiles(b)
                x_norm_step(b, 0)
                x_norm_step(b, 1)

        @block.scalar
        def _(act):
            act.wait_ge(w_in, 16 * N_W)

            def copy(dst, src, signal):
                act.activation(dst, src, ACT.Copy).then_inc(signal, 1)

            def s_front(b):
                act.wait_ge(s_tr, START + b + 1)
                act.wait_ge(s_proj, START + 3 * b)
                copy(xnT[:, :], mx_bank[0][:, :], mb_free[0])
                for i, part in ((0, q_part), (1, k_part)):
                    act.wait_ge(s_proj, START + 3 * b + 1 + i)
                    act.wait_ge(scr_out, START + 32 * b)
                    act.wait_ge(s_split, START + 6 * b)
                    ps = mx_bank[1 - i]
                    act.activation(qk_f[:, i, :], ps[:, :], ACT.Identity, bias=bcol[:, i:i + 1])
                    act.activation(part[:, 0, :], ps[:, :], ACT.Identity, bias=bcol[:, i:i + 1])\
                       .then_inc(mb_free[1 - i], 1)

            def s_max_row(b):
                act.wait_ge(mx_tr, START + b + 1)
                act.wait_ge(max_row, START + 32 * b)
                copy(mxT[:, :], s_bank[0:NPART * H, 0:N // 2].bitcast(BF16), sb_free)

            def s_exps(b):
                for t in range(TILES):
                    s = 3 * (t // TPG) + (0 if t % TPG < 4 else 1 if t % TPG < 8 else 2)
                    act.wait_ge(sc_ready, START + TILES * b + t + 1)
                    act.wait_ge(pv_done, START + 12 * b + max(s - 2, 0))
                    act.activation(Ps[:, t % TPG, :], sc_bank[t % 2][:, :], ACT.Exp, scale=SCALE)\
                       .then_inc(exp_done, 1)
                    if t == TILES // 2 + 3:
                        s_out(b, 0)
                s_out(b, 1)

            def s_out(b, half):
                act.wait_ge(pv_done, START + 12 * b + 6 * half + 6)
                act.wait_ge(n_tr, START + 4 * b)
                copy(Nh[:, half, :], s_bank[:, :], sb_free)

            def s_at(b):
                act.wait_ge(n_tr, START + 4 * b + 3)
                copy(atT[:, :], s_bank[:, :], sb_free)

            def c_keys(b):
                act.wait_ge(c_ready, START + 44 * b + 1)
                copy(cT[:, :], c_bank[0][:, 0:NK], c_free[0])
                act.wait_ge(c_ready, START + 44 * b + 2)
                act.wait_ge(xscr_out, START + 32 * b)
                act.activation(kx_f[:, :], c_bank[1][:, 0:NK], ACT.Identity, bias=bcol[:, 3:4])
                act.activation(kx_part[:, 0, :], c_bank[1][:, 0:NK], ACT.Identity, bias=bcol[:, 3:4])\
                   .then_inc(c_free[1], 1)

            def c_front(b):
                act.wait_ge(c_ready, START + 44 * b + 4)
                copy(xn2T[:, :], c_bank[1][:, :], c_free[1])
                act.wait_ge(c_ready, START + 44 * b + 5)
                act.activation(qx_f[:, :], c_bank[0][:, :], ACT.Identity, bias=bcol[:, 2:3])
                act.activation(qx_part[:, 0, :], c_bank[0][:, :], ACT.Identity, bias=bcol[:, 2:3])\
                   .then_inc(c_free[0], 1)

            def c_max_row(b):
                act.wait_ge(xb_ready, START + 9 * b + 1)
                act.wait_ge(xmax_row, START + 32 * b)
                copy(mxxT[:, :], x_bank[0:NPART * H, 0:N // 2].bitcast(BF16), xb_free)

            def c_exps(b):
                for t in range(H):
                    u = 17 + t
                    act.wait_ge(c_ready, START + 44 * b + u + 1)
                    act.wait_ge(xpv_done, START + 4 * b + max(t // 4 - 1, 0))
                    act.activation(Px[:, t % 8, :], c_bank[u % 2][:, :], ACT.Exp, scale=SCALE)\
                       .then_inc(c_free[u % 2], 1)
                    if t in (11, 15):
                        c_out(b, t // 15)

            def c_out(b, half):
                act.wait_ge(xpv_done, START + 4 * b + 2 * half + 2)
                copy(Nx[:, half, :], x_bank[:, :], xb_free)

            def experts(b):
                act.wait_ge(c_ready, START + 44 * b + 34)
                copy(xn2T[:, :], c_bank[1][:, :], c_free[1])
                act.wait_ge(xb_ready, START + 9 * b + 4)
                act.activation(eg[:, :, :], x_bank[:, 0:NT * E].rearrange("p (t e) -> p t e", e=E),
                               ACT.Exp, scale=-1.0).then_inc(xb_free, 1)
                act.wait_ge(xb_ready, START + 9 * b + 5)
                copy(combT[0:NPART * E, :], x_bank[0:NPART * E, 0:N // 2].bitcast(BF16), xb_free)
                for c in range(FC):
                    act.wait_ge(c_ready, START + 44 * b + 35 + 2 * c)
                    act.wait_ge(gate_done, START + 14 * b + (3 * (c - 2) + 1 if c >= 2 else 0))
                    act.activation(th[:, c % 2, :], c_bank[0][:, :], ACT.Tanh, scale=0.5).then_inc(tanh_done, 1)

            with act.Fori(0, B) as b:
                s_front(b)
                s_max_row(b)
                s_exps(b)
                s_at(b)
                c_keys(b)
                c_front(b)
                c_max_row(b)
                c_exps(b)
                experts(b)

        @block.vector
        def _(dve):
            for stack in (Ks, Qx, Kx):
                dve.memset(stack[ROWX:P, :, :].bitcast(F32), TWO_ONES)
            dve.memset(mask_s[:, 0, :], FAR).then_inc(mask_ready, 1)
            dve.wait_ge(mask_in, 48)
            dve.wait_ge(mask_ready, 1)
            dve.tensor_scalar(mask_s[:, 0, 0:NK], mask_i[:, :], 1.0, 10000.0 / SCALE,
                              ALU.subtract, ALU.mult).then_inc(mask_ready, 1)
            dve.wait_ge(mask_ready, 2)
            dve.tensor_copy(mask_b[:, 0, :], mask_s[:, 0, :]).then_inc(mask_ready, 1)
            dve.wait_ge(mask_ready, 3)
            dve.tensor_tensor(mask_s[:, 1, :], mask_s[:, 0, :], mask_b[:, 0, :], ALU.subtract)\
               .then_inc(mask_ready, 1)
            dve.wait_ge(mask_ready, 4)
            dve.tensor_copy(mask_b[:, 1, :], mask_s[:, 1, :]).then_inc(mask_ready, 1)
            dve.wait_ge(mask_ready, 5)
            dve.tensor_tensor(mask_b[:, 2, :], mask_s[:, 1, :], mask_b[:, 1, :], ALU.subtract)\
               .then_inc(mask_ready, 1)
            dve.wait_ge(w_in, 16 * N_W)
            dve.wait_ge(preset, 3)
            dve.tensor_copy(id_b[:, :], id_f[:, :])
            dve.tensor_copy(diag_b[:, :], diag_f[:, :])
            dve.tensor_copy(sel_b[:, :, :], sel_f[:, :, :]).then_inc(set_up, 1)

            def carry(i):
                dve.memset(spare[0:1, i:i + 1], 0.0)

            def norm(src, st, m, r, dst, steps, at, scale_sem, scale_at):
                for t in range(NT):
                    last = dve.bn_stats(st[:, t, :], src[:, t, :])
                last.then_inc(steps, 1)
                dve.wait_ge(steps, START + at + 1)
                carry(0)
                for t in range(NT):
                    last = dve.bn_aggr(m[:, t, :], st[:, t, :])
                last.then_inc(steps, 1)
                dve.wait_ge(steps, START + at + 2)
                dve.wait_ge(scale_sem, START + scale_at)
                for t in range(NT):
                    last = dve.tensor_scalar(dst[:, t, :], src[:, t, :], m[:, t, 0:1], r[:, t:t + 1],
                                             ALU.subtract, ALU.mult)
                last.then_inc(steps, 1)

            def s_front(b):
                dve.wait_ge(x_in, START + 16 * b + 16)
                dve.wait_ge(s_tr, START + b)
                norm(xin, stats, mv, rstd, xn, s_ln, 3 * b, s_rstd, 3 * b + 2)
                dve.wait_ge(scr_out, START + 32 * b)
                for i, part in ((0, q_part), (1, k_part)):
                    dve.wait_ge(mb_free[1 - i], START + 24 * b + 1 + i)
                    dve.tensor_tensor(qk_r[:, i, :], qk_f[:, i, :], part[:, 0, :], ALU.subtract)\
                       .then_inc(s_split, 1)
                for i, part in ((0, q_part), (1, k_part)):
                    dve.wait_ge(s_split, START + 6 * b + 1 + i)
                    dve.tensor_copy(part[:, 1, :], qk_r[:, i, :]).then_inc(s_split, 1)
                for i, part in ((0, q_part), (1, k_part)):
                    dve.wait_ge(s_split, START + 6 * b + 3 + i)
                    dve.tensor_tensor(part[:, 2, :], qk_r[:, i, :], part[:, 1, :], ALU.subtract)\
                       .then_inc(s_split, 1)
                dve.wait_ge(s_proj, START + 3 * b + 3)
                dve.wait_ge(pv_done, START + 12 * b)
                for e in range(2):
                    src = mx_bank[1][:, :].rearrange("p (t g e d) -> p t g e d", t=NT, e=2, d=DK)[:, :, :, e, :]
                    bv = brow[:, 0, :].rearrange("p (g e d) -> p g e d", e=2, d=DK)[:, :, e, :]
                    for t in range(NT):
                        last = dve.tensor_tensor(Vs[:, t, e:H:2, DK * e:DK * e + DK], src[:, t], bv, ALU.add)
                last.then_inc(mb_free[1], 1)

            def s_max(b):
                for n, (qt, h, k) in enumerate(MAX_TILES):
                    dve.wait_ge(max_ready, START + len(MAX_TILES) * b + n + 1)
                    if n == 0:
                        dve.wait_ge(mx_split, START + 4 * b)
                    w = P * (qt + 1)
                    dve.tensor_reduce(mx[:, qt, h:h + k],
                                      mx_bank[n % 2][:, 0:k * w].rearrange("p (h k) -> p h k", k=w),
                                      axis=AX_X, op=ALU.max, negate=True).then_inc(mb_free[n % 2], 1)
                dve.wait_ge(mb_free[0], START + 24 * b + 24)
                dve.wait_ge(mb_free[1], START + 24 * b + 24)
                dve.wait_ge(mx_tr, START + b)
                split(mx, mx_r, mx_part, mx_split, 4 * b)

            def split(src, rest, part, steps, at):
                dve.tensor_copy(part[:, :, 0, :], src[:, :, :]).then_inc(steps, 1)
                dve.wait_ge(steps, START + at + 1)
                dve.tensor_tensor(rest[:, :, :], src[:, :, :], part[:, :, 0, :], ALU.subtract).then_inc(steps, 1)
                dve.wait_ge(steps, START + at + 2)
                dve.tensor_copy(part[:, :, 1, :], rest[:, :, :]).then_inc(steps, 1)
                dve.wait_ge(steps, START + at + 3)
                dve.tensor_tensor(part[:, :, 2, :], rest[:, :, :], part[:, :, 1, :], ALU.subtract)\
                   .then_inc(steps, 1)

            def s_decay(b):
                for t in range(TILES):
                    if not on_pool(t):
                        kind = 0 if t % TPG < 4 else 1 if t % TPG < 8 else 2
                        dve.wait_ge(exp_done, START + TILES * b + t + 1)
                        dve.tensor_tensor(Ps[:, t % TPG, :], Ps[:, t % TPG, :], dec[:, kind, :],
                                          ALU.mult).then_inc(dec_dve, 1)

            def normalise(b, half, ps, d, dst, ready, ready_at, steps, steps_at, free):
                v = ps[:, :].rearrange("p (u c) -> p u c", c=32)
                dve.wait_ge(ready, START + ready_at)
                dve.wait_ge(steps, START + steps_at)
                dve.reciprocal(d[:, :, :], v[:, :, 16:32:8]).then_inc(steps, 1)
                dve.wait_ge(steps, START + steps_at + 1)
                for e in range(2):
                    to = dst[:, :, 64 * half:64 * half + 64].rearrange("p t (g c) -> p t g c", g=4)
                    last = dve.tensor_tensor(to[:, :, :, DK * e:DK * e + DK],
                                             v[:, :, DK * e:DK * e + DK].rearrange("p (t g) d -> p t g d", g=4),
                                             d[:, :, e:e + 1].rearrange("p (t g) o -> p t g o", g=4)
                                             .broadcast_to([P, NT, 4, DK]), ALU.mult)
                last.then_inc(free, 1)

            def s_tail(b):
                for half in range(2):
                    if half:
                        dve.wait_ge(sb_free, START + 7 * b + 4)
                    normalise(b, half, s_bank, den, at, n_tr, 4 * b + 1 + half, s_norm, 2 * b + half, sb_free)
                dve.wait_ge(n_tr, START + 4 * b + 4)
                dve.wait_ge(s_rstd, START + 3 * b + 3)
                dve.wait_ge(x_norm, START + 3 * b)
                dve.tensor_tensor(x1[:, :, :], s_bank[:, :].rearrange("p (t d) -> p t d", d=P),
                                  xb[:, :, :], ALU.add).then_inc(sb_free, 1)

            def c_keys(b):
                dve.wait_ge(c_free[1], START + 17 * b + 1)
                dve.tensor_tensor(kx_r[:, :], kx_f[:, :], kx_part[:, 0, :], ALU.subtract).then_inc(x_split, 1)
                dve.wait_ge(x_split, START + 6 * b + 1)
                dve.tensor_copy(kx_part[:, 1, :], kx_r[:, :]).then_inc(x_split, 1)
                dve.wait_ge(x_split, START + 6 * b + 2)
                dve.tensor_tensor(kx_part[:, 2, :], kx_r[:, :], kx_part[:, 1, :], ALU.subtract)\
                   .then_inc(x_split, 1)
                dve.wait_ge(c_ready, START + 44 * b + 3)
                dve.wait_ge(xpv_done, START + 4 * b)
                for e in range(2):
                    src = c_bank[0][0:NK, 0:P].rearrange("p (g e d) -> p g e d", e=2, d=DK)[:, :, e, :]
                    bv = brow[0:NK, 2, :].rearrange("p (g e d) -> p g e d", e=2, d=DK)[:, :, e, :]
                    last = dve.tensor_tensor(Vx[0:NK, e:H:2, DK * e:DK * e + DK], src, bv, ALU.add)
                last.then_inc(c_free[0], 1)

            def c_front(b):
                dve.wait_ge(sb_free, START + 7 * b + 7)
                norm(x1, statsx, mvx, rstdx, xn2, x_ln, 6 * b, x_rstd, 4 * b + 2)
                dve.wait_ge(c_free[0], START + 17 * b + 3)
                dve.tensor_tensor(qx_r[:, :], qx_f[:, :], qx_part[:, 0, :], ALU.subtract).then_inc(x_split, 1)
                dve.wait_ge(x_split, START + 6 * b + 4)
                dve.tensor_copy(qx_part[:, 1, :], qx_r[:, :]).then_inc(x_split, 1)
                dve.wait_ge(x_split, START + 6 * b + 5)
                dve.tensor_tensor(qx_part[:, 2, :], qx_r[:, :], qx_part[:, 1, :], ALU.subtract)\
                   .then_inc(x_split, 1)

            def c_max(b):
                for n, (qt, h, k) in enumerate(XMAX_TILES):
                    u = 5 + n
                    dve.wait_ge(c_ready, START + 44 * b + u + 1)
                    dve.tensor_reduce(mxx[:, qt, h:h + k],
                                      c_bank[u % 2][:, 0:k * NK].rearrange("p (h k) -> p h k", k=NK),
                                      axis=AX_X, op=ALU.max, negate=True).then_inc(c_free[u % 2], 1)
                dve.wait_ge(c_free[0], START + 17 * b + 9)
                dve.wait_ge(c_free[1], START + 17 * b + 8)
                split(mxx, mxx_r, mxx_part, xmx_split, 4 * b)

            def c_tail(b):
                for half in range(2):
                    if half:
                        dve.wait_ge(xb_free, START + 7 * b + 4)
                    normalise(b, half, x_bank, denx, atx, xb_ready, 9 * b + 2 + half, x_norm,
                              3 * b + half, xb_free)
                dve.wait_ge(xb_free, START + 7 * b + 5)
                dve.tensor_tensor(x2[:, :, :], x1[:, :, :], atx[:, :, :], ALU.add).then_inc(x_norm, 1)
                dve.wait_ge(x_norm, START + 3 * b + 3)
                norm(x2, statsx, mvx, rstdx, xn2, x_ln, 6 * b + 3, x_rstd, 4 * b + 4)

            def routing(b):
                at = 12 * b
                dve.wait_ge(xb_free, START + 7 * b + 6)
                dve.tensor_scalar(sg[:, :, :], eg[:, :, :], 1.0, None, ALU.add).then_inc(g_step, 1)
                dve.wait_ge(g_step, START + at + 1)
                dve.reciprocal(eg[:, :, :], sg[:, :, :]).then_inc(g_step, 1)
                dve.wait_ge(g_step, START + at + 2)
                carry(1)
                for t in range(NT):
                    last = dve.max(top[:, t, :], eg[:, t, :])
                last.then_inc(g_step, 1)
                dve.wait_ge(g_step, START + at + 3)
                carry(2)
                for t in range(NT):
                    last = dve.max_index(topi[:, t, :], top[:, t, :], eg[:, t, :])
                dve.scalar_tensor_tensor(wsum[:, :, :], top[:, :, 0:1], 1e-20, top[:, :, 1:2], ALU.add, ALU.add)\
                   .then_inc(g_step, 1)
                dve.wait_ge(g_step, START + at + 4)
                dve.tensor_copy(topf[:, :, :], topi[:, :, 0:2])
                dve.reciprocal(wsum[:, :, :], wsum[:, :, :]).then_inc(g_step, 1)
                dve.wait_ge(g_step, START + at + 5)
                dve.scalar_tensor_tensor(topw[:, :, :], top[:, :, 0:2], ROUTE, wsum[:, :, :].broadcast_to([P, NT, 2]),
                                         ALU.mult, ALU.mult).then_inc(g_step, 1)
                dve.wait_ge(g_step, START + at + 6)
                for k in range(2):
                    for t in range(NT):
                        last = dve.tensor_scalar(comb[:, k, t, :], iota_sb[:, :], topf[:, t, k:k + 1],
                                                 topw[:, t, k:k + 1], ALU.is_equal, ALU.mult)
                last.then_inc(g_step, 1)
                dve.wait_ge(g_step, START + at + 7)
                dve.tensor_tensor(comb_f[:, :, :], comb[:, 0], comb[:, 1], ALU.add).then_inc(g_step, 1)
                dve.wait_ge(g_step, START + at + 8)
                split(comb_f, comb_r, comb_part, g_step, at + 8)

            def experts(b):
                for c in range(FC):
                    n = 14 * b + 3 * c
                    dve.wait_ge(tanh_done, START + FC * b + c + 1)
                    dve.scalar_tensor_tensor(ga[:, c % 2, :], th[:, c % 2, :], 1.0, c_bank[0][:, :],
                                             ALU.add, ALU.mult).then_inc(gate_done, 1)
                    dve.wait_ge(c_ready, START + 44 * b + 36 + 2 * c)
                    dve.wait_ge(gate_done, START + n + 1)
                    dve.scalar_tensor_tensor(hm[:, c, :], ga[:, c % 2, :], 0.5, c_bank[1][:, :],
                                             ALU.mult, ALU.mult).then_inc(gate_done, 1)
                    if c < FC - 1:
                        dve.wait_ge(xb_ready, START + 9 * b + 6 + c)
                        dve.wait_ge(gate_done, START + n + 2)
                        dve.tensor_tensor(hm[:, c, :], hm[:, c, :], x_bank[:, :], ALU.mult)\
                           .then_inc(gate_done, 1)
                dve.wait_ge(down_done, START + b + 1)
                dve.wait_ge(y_out, START + 16 * b)
                dve.tensor_tensor(yo[:, :, :], x_bank[:, :].rearrange("p (t d) -> p t d", d=P), x2[:, :, :],
                                  ALU.add).then_inc(y_ready, 1)

            with dve.Fori(0, B) as b:
                s_front(b)
                s_max(b)
                s_decay(b)
                s_tail(b)
                c_keys(b)
                c_front(b)
                c_max(b)
                c_tail(b)
                routing(b)
                experts(b)

        @block.tensor
        def _(pe):
            def mm(dst, lhsT, rhs, start=True, stop=True):
                return pe.matmul(dst, lhsT, rhs, start=start, stop=stop, skip_group_check=True)

            def s_front(b):
                pe.wait_ge(s_ln, START + 3 * b + 3)
                pe.wait_ge(mb_free[0], START + 24 * b)
                for t in range(NT):
                    last = pe.transpose(mx_bank[0][:, P * t:P * t + P], xn[:, t, :], id_f[:, :])
                last.then_inc(s_tr, 1)
                pe.wait_ge(mb_free[0], START + 24 * b + 1)
                pe.wait_ge(mb_free[1], START + 24 * b)
                mm(mx_bank[1][:, :], w_sb[:, WQ, :], xnT[:, :]).then_inc(s_proj, 1)
                mm(mx_bank[0][:, :], w_sb[:, WK, :], xnT[:, :]).then_inc(s_proj, 1)
                pe.wait_ge(mb_free[1], START + 24 * b + 1)
                for t in range(NT):
                    last = mm(mx_bank[1][:, P * t:P * t + P], xnT[:, P * t:P * t + P], w_sb[:, WV, :])
                last.then_inc(s_proj, 1)

            def s_max(b):
                pe.wait_ge(stack_in, START + 288 * b + 288)
                for n, (qt, h0, k) in enumerate(MAX_TILES):
                    w = P * (qt + 1)
                    pe.wait_ge(mb_free[n % 2], START + 24 * b + 2 + n // 2)
                    for i in range(k):
                        mm(mx_bank[n % 2][:, w * i:w * i + w], Qs[0:KM, h0 + i, P * qt:P * qt + P],
                           Ks[0:KM, h0 + i, 0:w], stop=False)
                        last = mm(mx_bank[n % 2][:, w * i + w - P:w * i + w], id_b[:, :], diag_b[:, :],
                                  start=False)
                    last.then_inc(max_ready, 1)
                pe.wait_ge(mx_split, START + 4 * b + 4)
                pe.wait_ge(sb_free, START + 7 * b)
                for t in range(NT):
                    last = pe.transpose(s_bank[:, P // 2 * t:P // 2 * (t + 1)].bitcast(BF16),
                                        mx_part[:, t].rearrange("p i h -> p (i h)"), id_b[:, :])
                last.then_inc(mx_tr, 1)

            def s_scores(b, t):
                half, e = GROUPS[t // TPG]
                if t >= 2:
                    pe.wait_ge(exp_done, START + TILES * b + t - 1)
                else:
                    pe.wait_ge(exp_done, START + TILES * b)
                for g, kt, c in PIECES[t % TPG]:
                    h = head(half, e, g)
                    w = N - P * kt
                    last = mm(sc_bank[t % 2][:, c:c + w], Ks[0:KS, h, P * kt:P * kt + P],
                              Qs[0:KS, h, P * kt:N])
                last.then_inc(sc_ready, 1)

            def s_values(b, s):
                half, e = GROUPS[s // 3]
                if s % 6 == 0:
                    pe.wait_ge(sb_free, START + 7 * b + 1 + s // 6)
                t1 = TPG * (s // 3) + SETS[s % 3][1] - 1
                pe.wait_ge(dec_dve, START + DVE_N * b + applied_before(t1, False))
                pe.wait_ge(dec_pool, START + POOL_N * b + applied_before(t1, True))
                pieces = [(i, *piece) for i in range(*SETS[s % 3]) for piece in PIECES[i]]
                for i, g, kt, c in sorted(pieces, key=lambda p: (p[2], p[1])):
                    h = head(half, e, g)
                    w = N - P * kt
                    last = mm(s_bank[32 * g:32 * g + 32, P * kt:N], Vs[:, kt, h, :], Ps[:, i, c:c + w],
                              start=(e == 0 and kt == 0), stop=(e == 1 and kt == 2))
                last.then_inc(pv_done, 1)

            def s_tail(b):
                for half in range(2):
                    pe.wait_ge(sb_free, START + 7 * b + 3 + half)
                    for t in range(NT):
                        last = pe.transpose(s_bank[:, P * t:P * t + P], Nh[:, half, P * t:P * t + P], id_f[:, :])
                    last.then_inc(n_tr, 1)
                pe.wait_ge(sb_free, START + 7 * b + 5)
                for t in range(NT):
                    last = pe.transpose(s_bank[:, P * t:P * t + P], at[:, t, :], id_f[:, :])
                last.then_inc(n_tr, 1)
                pe.wait_ge(sb_free, START + 7 * b + 6)
                for t in range(NT):
                    last = mm(s_bank[:, P * t:P * t + P], atT[:, P * t:P * t + P], w_sb[:, WO, :])
                last.then_inc(n_tr, 1)

            def c_use(b, u):
                pe.wait_ge(c_free[u % 2], START + 17 * b + u // 2)
                return c_bank[u % 2]

            def c_keys(b):
                pe.wait_ge(gate_done, START + 14 * b)
                ps = c_use(b, 0)
                pe.wait_ge(ctx_in_s, START + 16 * b + 16)
                pe.transpose(ps[:, 0:NK], cin[:, :], id_f[0:NK, 0:NK]).then_inc(c_ready, 1)
                pe.wait_ge(c_free[0], START + 17 * b + 1)
                ps = c_use(b, 1)
                mm(ps[:, 0:NK], w_sb[:, WXK, :], cT[:, :]).then_inc(c_ready, 1)
                ps = c_use(b, 2)
                mm(ps[0:NK, 0:P], cT[:, :], w_sb[:, WXV, :]).then_inc(c_ready, 1)

            def c_front(b):
                pe.wait_ge(x_ln, START + 6 * b + 3)
                ps = c_use(b, 3)
                for t in range(NT):
                    last = pe.transpose(ps[:, P * t:P * t + P], xn2[:, t, :], id_f[:, :])
                last.then_inc(c_ready, 1)
                pe.wait_ge(c_free[1], START + 17 * b + 2)
                ps = c_use(b, 4)
                mm(ps[:, :], w_sb[:, WXQ, :], xn2T[:, :]).then_inc(c_ready, 1)

            def c_max(b):
                pe.wait_ge(xk_in, START + 144 * b + 144)
                pe.wait_ge(mask_rows, START + 48 * b + 48)
                pe.wait_ge(xq_in, START + 144 * b + 144)
                for n, (qt, h0, k) in enumerate(XMAX_TILES):
                    ps = c_use(b, 5 + n)
                    for i in range(k):
                        last = mm(ps[:, NK * i:NK * i + NK], Qx[0:KMX, h0 + i, P * qt:P * qt + P],
                                  Kx[0:KMX, h0 + i, 0:NK])
                    last.then_inc(c_ready, 1)
                pe.wait_ge(xmx_split, START + 4 * b + 4)
                pe.wait_ge(y_ready, START + b)
                for t in range(NT):
                    last = pe.transpose(x_bank[:, P // 2 * t:P // 2 * (t + 1)].bitcast(BF16),
                                        mxx_part[:, t].rearrange("p i h -> p (i h)"), id_b[:, :])
                last.then_inc(xb_ready, 1)

            def c_attend(b):
                pe.wait_ge(xmax_row, START + 32 * b + 32)
                for s in range(5):
                    if s < 4:
                        for g in range(4):
                            u = 17 + 4 * s + g
                            ps = c_use(b, u)
                            h = head(s // 2, s % 2, g)
                            mm(ps[:, :], Kx[0:KSX, h, :], Qx[0:KSX, h, :]).then_inc(c_ready, 1)
                    if s:
                        v = s - 1
                        pe.wait_ge(c_free[0], START + 17 * b + 11 + 2 * v)
                        pe.wait_ge(c_free[1], START + 17 * b + 10 + 2 * v)
                        if v % 2 == 0:
                            pe.wait_ge(xb_free, START + 7 * b + 1 + v // 2)
                        for g in range(4):
                            last = mm(x_bank[32 * g:32 * g + 32, :], Vx[:, head(v // 2, v % 2, g), :],
                                      Px[:, 4 * (v % 2) + g, :], start=v % 2 == 0, stop=v % 2 == 1)
                        last.then_inc(xpv_done, 1)
                for half in range(2):
                    pe.wait_ge(xb_free, START + 7 * b + 3 + half)
                    for t in range(NT):
                        last = pe.transpose(x_bank[:, P * t:P * t + P], Nx[:, half, P * t:P * t + P], id_f[:, :])
                    last.then_inc(xb_ready, 1)

            def experts(b):
                pe.wait_ge(x_ln, START + 6 * b + 6)
                ps = c_use(b, 33)
                for t in range(NT):
                    last = pe.transpose(ps[:, P * t:P * t + P], xn2[:, t, :], id_f[:, :])
                last.then_inc(c_ready, 1)
                pe.wait_ge(c_free[1], START + 17 * b + 17)
                pe.wait_ge(xb_free, START + 7 * b + 5)
                for t in range(NT):
                    last = mm(x_bank[:, E * t:E * t + E], xn2T[:, P * t:P * t + P], gate_sb[:, :])
                last.then_inc(xb_ready, 1)
                for c in range(FC):
                    for k, w in enumerate((wg_sb, wu_sb)):
                        if c:
                            pe.wait_ge(gate_done, START + 14 * b + 3 * (c - 1) + 1 + k)
                        else:
                            pe.wait_ge(c_free[k], START + 17 * b + 17)
                        mm(c_bank[k][:, :], w[:, P * c:P * c + P], xn2T[:, :]).then_inc(c_ready, 1)
                    if c == 0:
                        pe.wait_ge(g_step, START + 12 * b + 12)
                        pe.wait_ge(xb_free, START + 7 * b + 6)
                        for t in range(NT):
                            last = pe.transpose(x_bank[:, P // 2 * t:P // 2 * (t + 1)].bitcast(BF16),
                                                comb_part[:, t].rearrange("p i e -> p (i e)"), id_b[:, :])
                        last.then_inc(xb_ready, 1)
                    if c < FC - 1:
                        if c:
                            pe.wait_ge(gate_done, START + 14 * b + 3 * c)
                        else:
                            pe.wait_ge(xb_free, START + 7 * b + 7)
                        mm(x_bank[:, :], sel_b[:, c, :], combT[:, :]).then_inc(xb_ready, 1)
                pe.wait_ge(gate_done, START + 14 * b + 14)
                for t in range(NT):
                    for c in range(FC):
                        last = mm(x_bank[:, P * t:P * t + P], hm[:, c, P * t:P * t + P], wd_sb[:, c, :],
                                  start=c == 0, stop=c == FC - 1)
                last.then_inc(down_done, 1)

            pe.wait_ge(w_in, 16 * N_W)
            pe.wait_ge(mask_in, 48)
            pe.wait_ge(preset, 3)
            pe.wait_ge(set_up, 1)
            with pe.Fori(0, B) as b:
                s_front(b)
                s_max(b)
                pe.wait_ge(max_row, START + 32 * b + 32)
                for s in range(13):
                    if s < 12:
                        for i in range(*SETS[s % 3]):
                            s_scores(b, TPG * (s // 3) + i)
                    if s:
                        s_values(b, s - 1)
                s_tail(b)
                c_keys(b)
                c_front(b)
                c_max(b)
                c_attend(b)
                experts(b)


def kernel(**inputs):
    import numpy as np
    import concourse.bacc as bacc
    from concourse.bass_utils import run_bass_kernel_spmd as run

    a = {k: np.ascontiguousarray(v) for k, v in inputs.items()}
    i, j = np.arange(P)[:, None], np.arange(P)[None, :]
    delta = np.arange(N)[None, :] - np.arange(P)[:, None]
    part_expert = np.arange(P)[:, None, None]
    column_expert = 2 * np.arange(4)[None, :, None] + np.arange(P)[None, None, :] // 64
    ffn = "L0_ffn_"
    arrays = {
        "x": a["x"], "ctx_in": a["ctx_1024"], "mask": a["mask_BxS2_ik0"],
        "wq": a["L0_attn_Wq"], "wk": a["L0_attn_Wk"], "wv": a["L0_attn_Wv"], "wo": a["L0_attn_Wo"],
        "wxq": a["L0_xattn_Wq"].T, "wxk": a["L0_xattn_Wk"].T, "wxv": a["L0_xattn_Wv"].T,
        "bias_cols": np.stack([a["L0_attn_bq"], a["L0_attn_bk"], a["L0_xattn_bq"], a["L0_xattn_bk"]]),
        "bias_rows": np.stack([a["L0_attn_bv"], a["L0_attn_bo"], a["L0_xattn_bv"]]),
        "wg": np.concatenate([a[ffn + "w_gate"].reshape(512, P), a[ffn + "ws_gate"]]).T,
        "wu": np.concatenate([a[ffn + "w_up"].reshape(512, P), a[ffn + "ws_up"]]).T,
        "wd": np.concatenate([a[ffn + "w_down"].transpose(0, 2, 1).reshape(4, P, P), a[ffn + "ws_down"].T[None]]),
        "gate": a[ffn + "gate_weight"].T,
        "ident": np.eye(P, dtype=np.float32),
        "diag": np.where(j > i, np.float32(FAR), np.float32(0)).astype(np.float32),
        "decay": np.where(delta < 0, 0.0, np.maximum(delta, 1).astype(np.float64) ** -0.25).astype(np.float32),
        "sel": np.where(part_expert < NPART * E, part_expert % E == column_expert, False).astype(np.float32),
        "iota": np.tile(np.arange(E, dtype=np.float32), (P, 1)),
    }
    arrays = {k: np.ascontiguousarray(v) for k, v in arrays.items()}
    nc = bacc.Bacc("TRN2", target_bir_lowering=False, num_devices=1)
    args = {k: nc.dram_tensor(k, v.shape, mybir.dt.from_np(v.dtype), kind="ExternalInput").ap()
            for k, v in arrays.items()}
    out = nc.dram_tensor("out", (B, N, P), F32, kind="ExternalOutput").ap()
    decoder_layer(nc, out=out, **args)
    return run(nc, [arrays], core_ids=[0]).results[0]["out"]
```

```python
import struct
from contextlib import ExitStack

import concourse.bass as bass
from concourse import mybir

ALU = mybir.AluOpType
ACT = mybir.ActivationFunctionType
AX_X = mybir.AxisListType.X
F32 = mybir.dt.float32
BF16 = mybir.dt.bfloat16
I32 = mybir.dt.int32
U32 = mybir.dt.uint32

P = 128
B = 4
N = 512
NT = N // P
H = 16
DK = P // H
NK = 77
E = 8
FC = 5
NPART = 3
QK = NPART * NPART * DK
ROWX = 96
KM = 96
KS = ROWX + NPART
KMX = ROWX + NPART
KSX = ROWX + 2 * NPART
SCALE = float(DK) ** -0.5
EPS = 1e-5
ROUTE = 2.5
TWO_ONES = struct.unpack("f", struct.pack("I", 0x3F803F80))[0]
START = 1
FAR = -1e30

MAX_TILES = [(qt, g, k) for qt, k in enumerate((4, 2, 1, 1)) for g in range(0, 4, k)]
NM = len(MAX_TILES)
XMAX_TILES = [(qt, h, n) for qt in range(NT) for h, n in ((0, 6), (6, 5), (11, 5))]
PIECES = ([[(g, 0, 0)] for g in range(4)]
          + [[(g, 1, 0), (g, 3, 384)] for g in range(4)]
          + [[(0, 2, 0), (1, 2, 256)], [(2, 2, 0), (3, 2, 256)]])
SETS = [(0, 4), (4, 8), (8, 10)]
GROUPS = [(half, e) for half in range(2) for e in range(2)]
EXPERT_SLOTS = {11: (0,), 12: (1, 2), 13: (3,), 14: (4,)}
SLOTS = 15
TPG = len(PIECES)
TILES = TPG * len(GROUPS)
POOL_TILES = (0, 3, 5, 8)


def heads(half, e):
    return slice(8 * half + e, 8 * half + 8, 2)


def head(half, e, g):
    return 8 * half + 2 * g + e


def on_pool(t):
    return t % TPG in POOL_TILES


def set_tiles(s):
    return range(TPG * (s // 3) + SETS[s % 3][0], TPG * (s // 3) + SETS[s % 3][1])


def applied_before(t, pool):
    return sum(on_pool(x) == pool for x in range(t + 1))


def kind_of(t):
    return 0 if t % TPG < 4 else 1 if t % TPG < 8 else 2


BANK_USES = (4 + 4 * (NM + 1)) // 2


def front_uses(b):
    return BANK_USES * b - 12 if not isinstance(b, int) or b else 0


def max_uses(b, grp, last=False):
    if grp == 0:
        return BANK_USES * b + 2
    return BANK_USES * b + 8 + 6 * (grp - 1) + (2 if grp > 1 and not last else 0)


def max_part(grp, k, last):
    if grp == 1 and not last:
        return (range(0), range(NM), range(0))[k]
    return (range(0, 5), range(5, NM), range(0))[k]


POOL_N, DVE_N = applied_before(TILES - 1, True), applied_before(TILES - 1, False)


def decoder_layer(nc, x, ctx_in, mask, wq, wk, wv, wo, wxq, wxk, wxv, bias_cols, bias_rows,
                  wg, wu, wd, gate, ident, diag, decay, sel, iota, out):
    x_v = x.rearrange("b (t p) d -> b p t d", p=P)
    out_v = out.rearrange("b (t p) d -> b p t d", p=P)

    ctx = ExitStack()
    with ctx:
        def sb(name, shape, dt=F32):
            return ctx.enter_context(nc.sbuf_tensor(name, shape, dt))

        def sem(name):
            s = ctx.enter_context(nc.semaphore(name))
            counted.append(s)
            return s

        counted = []

        q_scr = nc.dram_tensor("q_scr", (NPART, P, N), BF16, kind="Internal").ap()
        k_scr = nc.dram_tensor("k_scr", (NPART, P, N), BF16, kind="Internal").ap()
        qx_scr = nc.dram_tensor("qx_scr", (NPART, P, N), BF16, kind="Internal").ap()
        mask_scr = nc.dram_tensor("mask_scr", (NPART, B, P), BF16, kind="Internal").ap()
        mx_scr = nc.dram_tensor("mx_scr", (NPART * 4, N), BF16, kind="Internal").ap()
        mxx_scr = nc.dram_tensor("mxx_scr", (NPART * H, N), BF16, kind="Internal").ap()
        kx_scr = nc.dram_tensor("kx_scr", (NPART, P, NK), BF16, kind="Internal").ap()

        w_sb = sb("w_sb", [P, 7, P])
        WQ, WK, WV, WO, WXQ, WXK, WXV = range(7)
        bcol = sb("bcol", [P, 4])
        brow = sb("brow", [P, 3, P])
        wg_sb = sb("wg_sb", [P, FC * P])
        wu_sb = sb("wu_sb", [P, FC * P])
        wd_sb = sb("wd_sb", [P, FC, P])
        gate_sb = sb("gate_sb", [P, E])
        id_f = sb("id_f", [P, P])
        id_b = sb("id_b", [P, P], BF16)
        diag_f = sb("diag_f", [P, P])
        diag_b = sb("diag_b", [P, P], BF16)
        dec = sb("dec", [P, 3, N])
        sel_f = sb("sel_f", [P, 4, P])
        sel_b = sb("sel_b", [P, 4, P], BF16)
        iota_sb = sb("iota_sb", [P, E])
        spare = sb("spare", [P, 4])
        half_pow = sb("half_pow", [P, NT])
        eps_sb = sb("eps_sb", [P, NT])
        mask_i = sb("mask_i", [B, NK], I32)
        mask_s = sb("mask_s", [B, 2, P])
        mask_b = sb("mask_b", [B, NPART, P], BF16)

        xin = sb("xin", [P, NT, P])
        xb = sb("xb", [P, NT, P])
        stats = sb("stats", [P, NT, 6])
        mv = sb("mv", [P, NT, 2])
        ve = sb("ve", [P, NT])
        rstd = sb("rstd", [P, NT])
        xn = sb("xn", [P, NT, P])
        xnT = sb("xnT", [P, N])
        qk_f = sb("qk_f", [P, 2, N])
        qk_r = sb("qk_r", [P, 2, N])
        q_part = sb("q_part", [P, NPART, N], BF16)
        k_part = sb("k_part", [P, NPART, N], BF16)
        Qs = sb("Qs", [P, H, N], BF16)
        Ks = sb("Ks", [P, H, N], BF16)
        Vs = sb("Vs", [P, NT, H, 32])
        v_sb = sb("v_sb", [P, NT, P])
        mx = sb("mx", [P, NT, 4])
        mx_r = sb("mx_r", [P, NT, 4])
        mx_part = sb("mx_part", [P, NT, P // 4, 4], BF16)
        mxT = sb("mxT", [NPART * 4, N], BF16)
        Ps = sb("Ps", [P, TPG, N])
        Nh = sb("Nh", [P, 2, N])
        den = sb("den", [P, NT * 4, 2])
        at = sb("at", [P, NT, P])
        atT = sb("atT", [P, N])
        x1 = sb("x1", [P, NT, P])

        cin = sb("cin", [NK, P])
        cT = sb("cT", [P, NK])
        kx_f = sb("kx_f", [P, NK])
        kx_r = sb("kx_r", [P, NK])
        kx_part = sb("kx_part", [P, NPART, NK], BF16)
        Kx = sb("Kx", [P, H, P], BF16)
        Vx = sb("Vx", [P, H, 32])
        statsx = sb("statsx", [P, NT, 6])
        mvx = sb("mvx", [P, NT, 2])
        vex = sb("vex", [P, NT])
        rstdx = sb("rstdx", [P, NT])
        xn2 = sb("xn2", [P, NT, P])
        xn2T = sb("xn2T", [P, N])
        qx_f = sb("qx_f", [P, N])
        qx_r = sb("qx_r", [P, N])
        qx_part = sb("qx_part", [P, NPART, N], BF16)
        Qx = sb("Qx", [P, H, N], BF16)
        mxx = sb("mxx", [P, NT, H])
        mxx_r = sb("mxx_r", [P, NT, H])
        mxx_part = sb("mxx_part", [P, NT, P // H, H], BF16)
        mxxT = sb("mxxT", [NPART * H, N], BF16)
        Px = sb("Px", [P, 8, N])
        Nx = sb("Nx", [P, 2, N])
        denx = sb("denx", [P, NT * 4, 2])
        atx = sb("atx", [P, NT, P])
        x2 = sb("x2", [P, NT, P])
        eg = sb("eg", [P, NT, E])
        sg = sb("sg", [P, NT, E])
        top = sb("top", [P, NT, 8])
        topi = sb("topi", [P, NT, 8], U32)
        topf = sb("topf", [P, NT, 2])
        wsum = sb("wsum", [P, NT, 1])
        topw = sb("topw", [P, NT, 2])
        comb = sb("comb", [P, 2, NT, E])
        comb_f = sb("comb_f", [P, NT, E])
        comb_r = sb("comb_r", [P, NT, E])
        comb_part = sb("comb_part", [P, NT, P // E, E], BF16)
        combT = sb("combT", [P, N], BF16)
        th = sb("th", [P, 2, N])
        ga = sb("ga", [P, 2, N])
        hm = sb("hm", [P, FC, N])
        yo = sb("yo", [P, NT, P])

        bank = [ctx.enter_context(nc.psum_tensor(f"bank{i}", [P, N], F32)) for i in range(8)]
        sc_bank = bank[0:2]
        mx_bank = bank[2:4]
        s_bank = bank[4]
        c_bank = bank[5:7]
        x_bank = bank[7]

        w_in = sem("w_in")
        mask_in = sem("mask_in")
        set_up = sem("set_up")
        mask_ready = sem("mask_ready")
        mask_out = sem("mask_out")
        preset = sem("preset")

        counted.clear()
        x_in = sem("x_in")
        s_ln = sem("s_ln")
        s_rstd = sem("s_rstd")
        xb_done = sem("xb_done")
        v_in = sem("v_in")
        s_tr = sem("s_tr")
        s_proj = sem("s_proj")
        s_split = sem("s_split")
        scr_out = sem("scr_out")
        stack_in = [sem("stack_in0"), sem("stack_in1")]
        max_ready = sem("max_ready")
        mb_free = [sem("mb_free0"), sem("mb_free1")]
        mx_split = sem("mx_split")
        mx_tr = sem("mx_tr")
        max_row = sem("max_row")
        sc_ready = sem("sc_ready")
        exp_done = sem("exp_done")
        dec_dve = sem("dec_dve")
        dec_pool = sem("dec_pool")
        pv_done = sem("pv_done")
        sb_free = sem("sb_free")
        n_tr = sem("n_tr")
        s_norm = sem("s_norm")

        mask_rows = sem("mask_rows")
        ctx_in_s = sem("ctx_in_s")
        x_ln = sem("x_ln")
        x_rstd = sem("x_rstd")
        c_ready = sem("c_ready")
        c_free = [sem("c_free0"), sem("c_free1")]
        x_split = sem("x_split")
        xscr_out = sem("xscr_out")
        xk_in = sem("xk_in")
        xq_in = sem("xq_in")
        xmx_split = sem("xmx_split")
        xmax_row = sem("xmax_row")
        xpv_done = sem("xpv_done")
        xb_ready = sem("xb_ready")
        xb_free = sem("xb_free")
        x_norm = sem("x_norm")
        g_sig = sem("g_sig")
        g_step = sem("g_step")
        tanh_done = sem("tanh_done")
        gate_done = sem("gate_done")
        down_done = sem("down_done")
        y_ready = sem("y_ready")
        y_out = sem("y_out")

        with nc.Block() as start:
            @start.sync
            def _(sp):
                for s in counted:
                    sp.sem_inc(s, START)

        N_W = 7 + 4 + 3 + 11
        block = ctx.enter_context(nc.Block())

        @block.sync
        def _(sp):
            sp.dma_start(mask_i[:, :], mask).then_inc(mask_in, 16)
            for i, w in enumerate((wq, wk, wv, wo, wxq, wxk, wxv)):
                sp.dma_start(w_sb[:, i, :], w).then_inc(w_in, 16)
            for i in range(4):
                sp.dma_start(bcol[:, i:i + 1], bias_cols[i].rearrange("(d o) -> d o", o=1)).then_inc(w_in, 16)
            for i in range(3):
                sp.dma_start(brow[:, i, :], bias_rows[i].partition_broadcast(P)).then_inc(w_in, 16)
            sp.dma_start(id_f[:, :], ident).then_inc(w_in, 16)
            sp.dma_start(diag_f[:, :], diag).then_inc(w_in, 16)
            sp.dma_start(dec[:, 0, :], decay).then_inc(w_in, 16)
            sp.dma_start(dec[:, 1, 0:384], decay[:, 0:384]).then_inc(w_in, 16)
            sp.dma_start(dec[:, 1, 384:512], decay[:, 0:128]).then_inc(w_in, 16)
            sp.dma_start(dec[:, 2, 0:256], decay[:, 0:256]).then_inc(w_in, 16)
            sp.dma_start(dec[:, 2, 256:512], decay[:, 0:256]).then_inc(w_in, 16)
            sp.dma_start(sel_f[:, :, :], sel).then_inc(w_in, 16)
            sp.dma_start(iota_sb[:, :], iota).then_inc(w_in, 16)
            sp.dma_start(gate_sb[:, :], gate).then_inc(w_in, 16)
            sp.dma_start(wd_sb[:, :, :], wd.rearrange("c f h -> f c h")).then_inc(w_in, 16)
            sp.dma_start(wg_sb[:, :], wg).then_inc(mask_in, 16)
            sp.dma_start(wu_sb[:, :], wu).then_inc(mask_in, 16)

            def load_x(b):
                sp.wait_ge(xb_done, START + b)
                sp.wait_ge(s_ln, START + 3 * b)
                sp.dma_start(xin[:, :, :], x_v[b]).then_inc(x_in, 16)

            def parts_out(b):
                sp.wait_ge(s_split, START + 6 * b + 6)
                sp.dma_start(q_scr.rearrange("i r t -> r i t"), q_part[:, :, :]).then_inc(scr_out, 16)
                sp.dma_start(k_scr.rearrange("i r t -> r i t"), k_part[:, :, :]).then_inc(scr_out, 16)

            def stack_loads(half):
                for i in range(NPART):
                    for r in range(NPART):
                        row = DK * (NPART * i + r)
                        for stack, scr in ((Qs, q_scr[i]), (Ks, k_scr[r])):
                            sp.dma_start(stack[row:row + DK, 8 * half:8 * half + 8, :],
                                         scr.rearrange("(h d) t -> d h t", d=DK)[:, 8 * half:8 * half + 8, :])\
                              .then_inc(stack_in[half], 16)

            def stacks_in(b, half):
                sp.wait_ge(sc_ready, START + TILES * b - TILES // 2 * (1 - half))
                sp.wait_ge(scr_out, START + 32 * b + 32)
                stack_loads(half)

            def s_max_rows(b, grp, last):
                sp.wait_ge(mb_free[1], START + max_uses(b, grp, last) + NM // 2 + 1)
                sp.dma_start(mx_scr, mxT[:, :]).then_inc(max_row, 16)
                sp.wait_ge(max_row, START + 128 * b + 32 * grp + 16)
                sp.dma_start(Qs[ROWX:ROWX + NPART, heads(*GROUPS[grp]), :],
                             mx_scr.rearrange("(i h) t -> i h t", h=4)).then_inc(max_row, 16)

            def load_ctx(b):
                sp.wait_ge(c_ready, START + 44 * b)
                sp.dma_start(cin[:, :], ctx_in[b]).then_inc(ctx_in_s, 16)

            def mask_row(b):
                sp.wait_ge(xpv_done, START + 4 * b)
                for i in range(NPART):
                    sp.dma_start(Kx[ROWX + i:ROWX + i + 1, :, :],
                                 mask_scr[i:i + 1, bass.ds(b, 1), :].broadcast_to([1, H, P]))\
                      .then_inc(mask_rows, 16)

            def x_keys(b):
                sp.wait_ge(x_split, START + 6 * b + 3)
                sp.dma_start(kx_scr.rearrange("i r t -> r i t"), kx_part[:, :, :]).then_inc(xscr_out, 16)
                sp.wait_ge(xscr_out, START + 32 * b + 16)
                for i in range(NPART):
                    for r in range(NPART):
                        row = DK * (NPART * i + r)
                        sp.dma_start(Kx[row:row + DK, :, 0:NK],
                                     kx_scr[r].rearrange("(h d) t -> d h t", d=DK)).then_inc(xk_in, 16)

            def x_queries(b):
                sp.wait_ge(x_split, START + 6 * b + 6)
                sp.dma_start(qx_scr.rearrange("i r t -> r i t"), qx_part[:, :, :]).then_inc(xscr_out, 16)
                sp.wait_ge(xscr_out, START + 32 * b + 32)
                for i in range(NPART):
                    for r in range(NPART):
                        row = DK * (NPART * i + r)
                        sp.dma_start(Qx[row:row + DK, :, :],
                                     qx_scr[i].rearrange("(h d) t -> d h t", d=DK)).then_inc(xq_in, 16)

            def x_max_rows(b):
                sp.wait_ge(xb_free, START + 7 * b + 1)
                sp.dma_start(mxx_scr, mxxT[:, :]).then_inc(xmax_row, 16)
                sp.wait_ge(xmax_row, START + 32 * b + 16)
                sp.dma_start(Qx[ROWX + NPART:ROWX + 2 * NPART, :, :], mxx_scr.rearrange("(i h) t -> i h t", h=H))\
                  .then_inc(xmax_row, 16)

            def store_y(b):
                sp.wait_ge(y_ready, START + b + 1)
                sp.dma_start(out_v[b], yo[:, :, :]).then_inc(y_out, 16)

            sp.wait_ge(preset, 1)
            sp.wait_ge(mask_ready, 6)
            sp.dma_start(mask_scr.rearrange("i b k -> b i k"), mask_b[:, :, :]).then_inc(mask_out, 16)
            sp.wait_ge(mask_out, 16)

            def c_slot(b, i):
                if i == 0:
                    load_ctx(b)
                    mask_row(b)
                elif i == 1:
                    x_keys(b)
                elif i == 2:
                    x_queries(b)
                elif i == 4:
                    x_max_rows(b)
                elif i == 14:
                    store_y(b)

            def step(b, cb, last=False):
                for grp in range(4):
                    for k in range(3):
                        i = 3 * grp + k
                        if k == 2 and not (last and grp == 3):
                            s_max_rows(b + (grp == 3), (grp + 1) % 4, last)
                        if not last:
                            if i == 0:
                                load_x(b + 1)
                            elif i == 4:
                                parts_out(b + 1)
                            elif i == 6:
                                stacks_in(b + 1, 0)
                        if cb is not None:
                            c_slot(cb, i)
                if not last:
                    stacks_in(b + 1, 1)
                for i in range(12, SLOTS):
                    if cb is not None:
                        c_slot(cb, i)

            load_x(0)
            parts_out(0)
            sp.wait_ge(scr_out, START + 32)
            stack_loads(0)
            stack_loads(1)
            s_max_rows(0, 0, False)
            step(0, None)
            with sp.Fori(1, B - 1) as b:
                step(b, b - 1)
            step(B - 1, B - 2, last=True)
            for i in range(SLOTS):
                c_slot(B - 1, i)
            sp.wait_ge(y_out, START + 16 * B)

        @block.gpsimd
        def _(pool):
            for stack in (Qs, Ks, Qx, Kx):
                pool.memset(stack[0:ROWX, :, :].bitcast(F32), 0.0)
            pool.memset(Vs[:, :, :, :], 0.0)
            pool.memset(Vx[:, :, :], 0.0)
            pool.memset(combT[:, :], 0.0)
            for part in (mx_part, mxx_part, comb_part):
                pool.memset(part[:, :, :, :], 0.0)
            pool.memset(eps_sb[:, :], EPS)
            pool.memset(half_pow[:, :], -0.5).then_inc(preset, 1)
            pool.wait_ge(preset, 1)
            for e in range(2):
                pool.memset(Vs[:, :, e:H:2, 16 + 8 * e:24 + 8 * e], 1.0)
                pool.memset(Vx[:, e:H:2, 16 + 8 * e:24 + 8 * e], 1.0).then_inc(preset, 1)
            pool.wait_ge(w_in, 16 * N_W)
            pool.wait_ge(preset, 3)

            def s_norm_step(b):
                pool.wait_ge(s_ln, START + 3 * b + 2)
                pool.tensor_tensor(ve[:, :], mv[:, :, 1], eps_sb[:, :], ALU.add).then_inc(s_rstd, 1)
                pool.wait_ge(s_rstd, START + 2 * b + 1)
                pool.tensor_tensor(rstd[:, :], ve[:, :], half_pow[:, :], ALU.pow).then_inc(s_rstd, 1)

            def s_bias(b):
                pool.wait_ge(x_in, START + 16 * b + 16)
                pool.wait_ge(sb_free, START + 6 * b)
                pool.tensor_tensor(xb[:, :, :], xin[:, :, :], brow[:, 1:2, :].broadcast_to([P, NT, P]),
                                   ALU.add).then_inc(xb_done, 1)

            def s_values_in(b):
                pool.wait_ge(mb_free[1], START + front_uses(b) + 2)
                pool.wait_ge(pv_done, START + 12 * b)
                for e in range(2):
                    for t in range(NT):
                        v = v_sb[:, t].rearrange("p (g e d) -> p g e d", e=2, d=DK)[:, :, e, :]
                        bv = brow[:, 0].rearrange("p (g e d) -> p g e d", e=2, d=DK)[:, :, e, :]
                        last = pool.tensor_tensor(Vs[:, t, e:H:2, DK * e:DK * e + DK], v, bv, ALU.add)
                last.then_inc(v_in, 1)

            def x_norm_step(b, k):
                pool.wait_ge(x_ln, START + 6 * b + 3 * k + 2)
                pool.tensor_tensor(vex[:, :], mvx[:, :, 1], eps_sb[:, :], ALU.add).then_inc(x_rstd, 1)
                pool.wait_ge(x_rstd, START + 4 * b + 2 * k + 1)
                pool.tensor_tensor(rstdx[:, :], vex[:, :], half_pow[:, :], ALU.pow).then_inc(x_rstd, 1)

            def decay_tiles(b, s):
                for t in set_tiles(s):
                    if on_pool(t):
                        pool.wait_ge(exp_done, START + TILES * b + t + 1)
                        pool.tensor_tensor(Ps[:, t % TPG, :], Ps[:, t % TPG, :], dec[:, kind_of(t), :],
                                           ALU.mult).then_inc(dec_pool, 1)

            def c_slot(b, i):
                if i in (0, 9):
                    x_norm_step(b, i // 9)

            def step(b, cb, last=False):
                s_bias(b)
                for i in range(12):
                    decay_tiles(b, i)
                    if i == 2 and not last:
                        s_norm_step(b + 1)
                    if cb is not None:
                        c_slot(cb, i)
                if not last:
                    s_values_in(b + 1)
                for i in range(12, SLOTS):
                    if cb is not None:
                        c_slot(cb, i)

            s_norm_step(0)
            s_values_in(0)
            step(0, None)
            with pool.Fori(1, B - 1) as b:
                step(b, b - 1)
            step(B - 1, B - 2, last=True)
            for i in range(SLOTS):
                c_slot(B - 1, i)

        @block.scalar
        def _(act):
            act.wait_ge(w_in, 16 * N_W)

            def copy(dst, src, signal):
                act.activation(dst, src, ACT.Copy).then_inc(signal, 1)

            def s_front(b):
                act.wait_ge(s_tr, START + b + 1)
                act.wait_ge(s_proj, START + 3 * b)
                copy(xnT[:, :], mx_bank[0][:, :], mb_free[0])
                for i, part in ((0, q_part), (1, k_part)):
                    act.wait_ge(s_proj, START + 3 * b + 1 + i)
                    act.wait_ge(scr_out, START + 32 * b)
                    act.wait_ge(s_split, START + 6 * b)
                    ps = mx_bank[1 - i]
                    act.activation(qk_f[:, i, :], ps[:, :], ACT.Identity, bias=bcol[:, i:i + 1])
                    act.activation(part[:, 0, :], ps[:, :], ACT.Identity, bias=bcol[:, i:i + 1])\
                       .then_inc(mb_free[1 - i], 1)

            def s_max_row(b, grp):
                act.wait_ge(mx_tr, START + 4 * b + grp + 1)
                act.wait_ge(max_row, START + 128 * b + 32 * grp)
                copy(mxT[:, :], mx_bank[1][0:NPART * 4, 0:N // 2].bitcast(BF16), mb_free[1])

            def s_exps(b, s):
                for t in set_tiles(s):
                    act.wait_ge(sc_ready, START + TILES * b + t + 1)
                    act.wait_ge(pv_done, START + 12 * b + max(s - 2, 0))
                    act.activation(Ps[:, t % TPG, :], sc_bank[t % 2][:, :], ACT.Exp, scale=SCALE)\
                       .then_inc(exp_done, 1)

            def s_out(b, half):
                act.wait_ge(pv_done, START + 12 * b + 6 * half + 6)
                act.wait_ge(n_tr, START + 4 * b)
                copy(Nh[:, half, :], s_bank[:, :], sb_free)

            def s_at(b):
                act.wait_ge(n_tr, START + 4 * b + 3)
                copy(atT[:, :], s_bank[:, :], sb_free)

            def c_keys(b):
                act.wait_ge(c_ready, START + 44 * b + 1)
                copy(cT[:, :], c_bank[0][:, 0:NK], c_free[0])
                act.wait_ge(c_ready, START + 44 * b + 2)
                act.wait_ge(xscr_out, START + 32 * b)
                act.activation(kx_f[:, :], c_bank[1][:, 0:NK], ACT.Identity, bias=bcol[:, 3:4])
                act.activation(kx_part[:, 0, :], c_bank[1][:, 0:NK], ACT.Identity, bias=bcol[:, 3:4])\
                   .then_inc(c_free[1], 1)

            def c_front(b):
                act.wait_ge(c_ready, START + 44 * b + 4)
                copy(xn2T[:, :], c_bank[1][:, :], c_free[1])
                act.wait_ge(c_ready, START + 44 * b + 5)
                act.activation(qx_f[:, :], c_bank[0][:, :], ACT.Identity, bias=bcol[:, 2:3])
                act.activation(qx_part[:, 0, :], c_bank[0][:, :], ACT.Identity, bias=bcol[:, 2:3])\
                   .then_inc(c_free[0], 1)

            def c_max_row(b):
                act.wait_ge(xb_ready, START + 9 * b + 1)
                act.wait_ge(xmax_row, START + 32 * b)
                copy(mxxT[:, :], x_bank[0:NPART * H, 0:N // 2].bitcast(BF16), xb_free)

            def c_exps(b, s):
                for t in range(4 * s, 4 * s + 4):
                    u = 17 + t
                    act.wait_ge(c_ready, START + 44 * b + u + 1)
                    act.wait_ge(xpv_done, START + 4 * b + max(t // 4 - 1, 0))
                    act.activation(Px[:, t % 8, :], c_bank[u % 2][:, :], ACT.Exp, scale=SCALE)\
                       .then_inc(c_free[u % 2], 1)

            def c_out(b, half):
                act.wait_ge(xpv_done, START + 4 * b + 2 * half + 2)
                copy(Nx[:, half, :], x_bank[:, :], xb_free)

            def experts_in(b):
                act.wait_ge(c_ready, START + 44 * b + 34)
                copy(xn2T[:, :], c_bank[1][:, :], c_free[1])
                act.wait_ge(xb_ready, START + 9 * b + 4)
                act.activation(eg[:, :, :], x_bank[:, 0:NT * E].rearrange("p (t e) -> p t e", e=E),
                               ACT.Exp, scale=-1.0).then_inc(xb_free, 1)

            def expert(b, c):
                act.wait_ge(c_ready, START + 44 * b + 35 + 2 * c)
                act.wait_ge(gate_done, START + 14 * b + (3 * (c - 2) + 1 if c >= 2 else 0))
                act.activation(th[:, c % 2, :], c_bank[0][:, :], ACT.Tanh, scale=0.5).then_inc(tanh_done, 1)
                if c == 0:
                    act.wait_ge(xb_ready, START + 9 * b + 5)
                    copy(combT[0:NPART * E, :], x_bank[0:NPART * E, 0:N // 2].bitcast(BF16), xb_free)

            def c_slot(b, i):
                if i == 1:
                    c_keys(b)
                    c_front(b)
                elif i == 4:
                    c_max_row(b)
                elif 5 <= i < 9:
                    c_exps(b, i - 5)
                    if i == 7:
                        c_out(b, 0)
                elif i == 9:
                    c_out(b, 1)
                elif i == 10:
                    experts_in(b)
                elif i in EXPERT_SLOTS:
                    for c in EXPERT_SLOTS[i]:
                        expert(b, c)

            def step(b, cb, last=False):
                for grp in range(4):
                    for k in range(3):
                        i = 3 * grp + k
                        if k == 2 and not (last and grp == 3):
                            s_max_row(b + (grp == 3), (grp + 1) % 4)
                        s_exps(b, i)
                        if i == 6:
                            s_out(b, 0)
                        if i == 3 and not last:
                            s_front(b + 1)
                        if cb is not None:
                            c_slot(cb, i)
                s_out(b, 1)
                if cb is not None:
                    c_slot(cb, 12)
                s_at(b)
                for i in range(13, SLOTS):
                    if cb is not None:
                        c_slot(cb, i)

            s_front(0)
            s_max_row(0, 0)
            step(0, None)
            with act.Fori(1, B - 1) as b:
                step(b, b - 1)
            step(B - 1, B - 2, last=True)
            for i in range(SLOTS):
                c_slot(B - 1, i)

        @block.vector
        def _(dve):
            for stack in (Ks, Qx, Kx):
                dve.memset(stack[ROWX:P, :, :].bitcast(F32), TWO_ONES)
            dve.memset(mask_s[:, 0, :], FAR).then_inc(mask_ready, 1)
            dve.wait_ge(mask_in, 48)
            dve.wait_ge(mask_ready, 1)
            dve.tensor_scalar(mask_s[:, 0, 0:NK], mask_i[:, :], 1.0, 10000.0 / SCALE,
                              ALU.subtract, ALU.mult).then_inc(mask_ready, 1)
            dve.wait_ge(mask_ready, 2)
            dve.tensor_copy(mask_b[:, 0, :], mask_s[:, 0, :]).then_inc(mask_ready, 1)
            dve.wait_ge(mask_ready, 3)
            dve.tensor_tensor(mask_s[:, 1, :], mask_s[:, 0, :], mask_b[:, 0, :], ALU.subtract)\
               .then_inc(mask_ready, 1)
            dve.wait_ge(mask_ready, 4)
            dve.tensor_copy(mask_b[:, 1, :], mask_s[:, 1, :]).then_inc(mask_ready, 1)
            dve.wait_ge(mask_ready, 5)
            dve.tensor_tensor(mask_b[:, 2, :], mask_s[:, 1, :], mask_b[:, 1, :], ALU.subtract)\
               .then_inc(mask_ready, 1)
            dve.wait_ge(w_in, 16 * N_W)
            dve.wait_ge(preset, 3)
            dve.tensor_copy(id_b[:, :], id_f[:, :])
            dve.tensor_copy(diag_b[:, :], diag_f[:, :])
            dve.tensor_copy(sel_b[:, :, :], sel_f[:, :, :]).then_inc(set_up, 1)

            def carry(i):
                dve.memset(spare[0:1, i:i + 1], 0.0)

            def norm_stats(src, st, m, steps, at):
                for t in range(NT):
                    last = dve.bn_stats(st[:, t, :], src[:, t, :])
                last.then_inc(steps, 1)
                dve.wait_ge(steps, START + at + 1)
                carry(0)
                for t in range(NT):
                    last = dve.bn_aggr(m[:, t, :], st[:, t, :])
                last.then_inc(steps, 1)

            def norm_apply(src, m, r, dst, steps, at, scale_sem, scale_at):
                dve.wait_ge(steps, START + at + 2)
                dve.wait_ge(scale_sem, START + scale_at)
                for t in range(NT):
                    last = dve.tensor_scalar(dst[:, t, :], src[:, t, :], m[:, t, 0:1], r[:, t:t + 1],
                                             ALU.subtract, ALU.mult)
                last.then_inc(steps, 1)

            def s_stats(b):
                dve.wait_ge(x_in, START + 16 * b + 16)
                norm_stats(xin, stats, mv, s_ln, 3 * b)

            def s_apply(b):
                dve.wait_ge(s_tr, START + b)
                norm_apply(xin, mv, rstd, xn, s_ln, 3 * b, s_rstd, 2 * b + 2)

            def s_front(b):
                n = front_uses(b)
                dve.wait_ge(scr_out, START + 32 * b)
                for i, part in ((0, q_part), (1, k_part)):
                    dve.wait_ge(mb_free[1 - i], START + n + 1 + i)
                    dve.tensor_tensor(qk_r[:, i, :], qk_f[:, i, :], part[:, 0, :], ALU.subtract)\
                       .then_inc(s_split, 1)
                for i, part in ((0, q_part), (1, k_part)):
                    dve.wait_ge(s_split, START + 6 * b + 1 + i)
                    dve.tensor_copy(part[:, 1, :], qk_r[:, i, :]).then_inc(s_split, 1)
                for i, part in ((0, q_part), (1, k_part)):
                    dve.wait_ge(s_split, START + 6 * b + 3 + i)
                    dve.tensor_tensor(part[:, 2, :], qk_r[:, i, :], part[:, 1, :], ALU.subtract)\
                       .then_inc(s_split, 1)
                dve.wait_ge(s_proj, START + 3 * b + 3)
                dve.wait_ge(v_in, START + b)
                dve.tensor_copy(v_sb[:, :, :], mx_bank[1][:, :].rearrange("p (t d) -> p t d", d=P))\
                   .then_inc(mb_free[1], 1)

            def s_max(b, grp, part, last):
                base = max_uses(b, grp, last)
                for n in part:
                    qt, g, k = MAX_TILES[n]
                    dve.wait_ge(max_ready, START + 4 * NM * b + NM * grp + n + 1)
                    if n == 0:
                        dve.wait_ge(mx_split, START + 16 * b + 4 * grp)
                    w = P * (qt + 1)
                    dve.tensor_reduce(mx[:, qt, g:g + k],
                                      mx_bank[n % 2][:, 0:k * w].rearrange("p (h k) -> p h k", k=w),
                                      axis=AX_X, op=ALU.max, negate=True).then_inc(mb_free[n % 2], 1)
                if NM - 1 in part:
                    dve.wait_ge(mb_free[0], START + base + (NM + 1) // 2)
                    dve.wait_ge(mb_free[1], START + base + NM // 2)
                    dve.wait_ge(mx_tr, START + 4 * b + grp)
                    split(mx, mx_r, mx_part, mx_split, 16 * b + 4 * grp)

            def split(src, rest, part, steps, at):
                dve.tensor_copy(part[:, :, 0, :], src[:, :, :]).then_inc(steps, 1)
                dve.wait_ge(steps, START + at + 1)
                dve.tensor_tensor(rest[:, :, :], src[:, :, :], part[:, :, 0, :], ALU.subtract).then_inc(steps, 1)
                dve.wait_ge(steps, START + at + 2)
                dve.tensor_copy(part[:, :, 1, :], rest[:, :, :]).then_inc(steps, 1)
                dve.wait_ge(steps, START + at + 3)
                dve.tensor_tensor(part[:, :, 2, :], rest[:, :, :], part[:, :, 1, :], ALU.subtract)\
                   .then_inc(steps, 1)

            def s_decay(b, s):
                for t in set_tiles(s):
                    if not on_pool(t):
                        dve.wait_ge(exp_done, START + TILES * b + t + 1)
                        dve.tensor_tensor(Ps[:, t % TPG, :], Ps[:, t % TPG, :], dec[:, kind_of(t), :],
                                          ALU.mult).then_inc(dec_dve, 1)

            def normalise(b, half, ps, d, dst, ready, ready_at, steps, steps_at, free):
                v = ps[:, :].rearrange("p (u c) -> p u c", c=32)
                dve.wait_ge(ready, START + ready_at)
                dve.wait_ge(steps, START + steps_at)
                dve.reciprocal(d[:, :, :], v[:, :, 16:32:8]).then_inc(steps, 1)
                dve.wait_ge(steps, START + steps_at + 1)
                for e in range(2):
                    to = dst[:, :, 64 * half:64 * half + 64].rearrange("p t (g c) -> p t g c", g=4)
                    last = dve.tensor_tensor(to[:, :, :, DK * e:DK * e + DK],
                                             v[:, :, DK * e:DK * e + DK].rearrange("p (t g) d -> p t g d", g=4),
                                             d[:, :, e:e + 1].rearrange("p (t g) o -> p t g o", g=4)
                                             .broadcast_to([P, NT, 4, DK]), ALU.mult)
                last.then_inc(free, 1)

            def s_tail(b, half):
                if half:
                    dve.wait_ge(sb_free, START + 6 * b + 3)
                normalise(b, half, s_bank, den, at, n_tr, 4 * b + 1 + half, s_norm, 2 * b + half, sb_free)

            def s_result(b):
                dve.wait_ge(n_tr, START + 4 * b + 4)
                dve.wait_ge(xb_done, START + b + 1)
                dve.wait_ge(x_norm, START + 3 * b)
                dve.tensor_tensor(x1[:, :, :], s_bank[:, :].rearrange("p (t d) -> p t d", d=P),
                                  xb[:, :, :], ALU.add).then_inc(sb_free, 1)

            def c_keys(b):
                dve.wait_ge(c_free[1], START + 17 * b + 1)
                dve.tensor_tensor(kx_r[:, :], kx_f[:, :], kx_part[:, 0, :], ALU.subtract).then_inc(x_split, 1)
                dve.wait_ge(x_split, START + 6 * b + 1)
                dve.tensor_copy(kx_part[:, 1, :], kx_r[:, :]).then_inc(x_split, 1)
                dve.wait_ge(x_split, START + 6 * b + 2)
                dve.tensor_tensor(kx_part[:, 2, :], kx_r[:, :], kx_part[:, 1, :], ALU.subtract)\
                   .then_inc(x_split, 1)
                dve.wait_ge(c_ready, START + 44 * b + 3)
                dve.wait_ge(xpv_done, START + 4 * b)
                for e in range(2):
                    src = c_bank[0][0:NK, 0:P].rearrange("p (g e d) -> p g e d", e=2, d=DK)[:, :, e, :]
                    bv = brow[0:NK, 2, :].rearrange("p (g e d) -> p g e d", e=2, d=DK)[:, :, e, :]
                    last = dve.tensor_tensor(Vx[0:NK, e:H:2, DK * e:DK * e + DK], src, bv, ALU.add)
                last.then_inc(c_free[0], 1)

            def c_stats(b):
                dve.wait_ge(sb_free, START + 6 * b + 6)
                norm_stats(x1, statsx, mvx, x_ln, 6 * b)

            def c_apply(b):
                norm_apply(x1, mvx, rstdx, xn2, x_ln, 6 * b, x_rstd, 4 * b + 2)

            def c_front(b):
                dve.wait_ge(c_free[0], START + 17 * b + 3)
                dve.tensor_tensor(qx_r[:, :], qx_f[:, :], qx_part[:, 0, :], ALU.subtract).then_inc(x_split, 1)
                dve.wait_ge(x_split, START + 6 * b + 4)
                dve.tensor_copy(qx_part[:, 1, :], qx_r[:, :]).then_inc(x_split, 1)
                dve.wait_ge(x_split, START + 6 * b + 5)
                dve.tensor_tensor(qx_part[:, 2, :], qx_r[:, :], qx_part[:, 1, :], ALU.subtract)\
                   .then_inc(x_split, 1)

            def c_max(b):
                for n, (qt, h, k) in enumerate(XMAX_TILES):
                    u = 5 + n
                    dve.wait_ge(c_ready, START + 44 * b + u + 1)
                    dve.tensor_reduce(mxx[:, qt, h:h + k],
                                      c_bank[u % 2][:, 0:k * NK].rearrange("p (h k) -> p h k", k=NK),
                                      axis=AX_X, op=ALU.max, negate=True).then_inc(c_free[u % 2], 1)
                dve.wait_ge(c_free[0], START + 17 * b + 9)
                dve.wait_ge(c_free[1], START + 17 * b + 8)
                split(mxx, mxx_r, mxx_part, xmx_split, 4 * b)

            def c_tail(b):
                for half in range(2):
                    if half:
                        dve.wait_ge(xb_free, START + 7 * b + 4)
                    normalise(b, half, x_bank, denx, atx, xb_ready, 9 * b + 2 + half, x_norm,
                              3 * b + half, xb_free)
                dve.wait_ge(xb_free, START + 7 * b + 5)
                dve.tensor_tensor(x2[:, :, :], x1[:, :, :], atx[:, :, :], ALU.add).then_inc(x_norm, 1)
                dve.wait_ge(x_norm, START + 3 * b + 3)
                norm_stats(x2, statsx, mvx, x_ln, 6 * b + 3)

            def routing(b):
                at = 12 * b
                dve.wait_ge(xb_free, START + 7 * b + 6)
                dve.tensor_scalar(sg[:, :, :], eg[:, :, :], 1.0, None, ALU.add).then_inc(g_step, 1)
                dve.wait_ge(g_step, START + at + 1)
                dve.reciprocal(eg[:, :, :], sg[:, :, :]).then_inc(g_step, 1)
                dve.wait_ge(g_step, START + at + 2)
                carry(1)
                for t in range(NT):
                    last = dve.max(top[:, t, :], eg[:, t, :])
                last.then_inc(g_step, 1)
                dve.wait_ge(g_step, START + at + 3)
                carry(2)
                for t in range(NT):
                    last = dve.max_index(topi[:, t, :], top[:, t, :], eg[:, t, :])
                dve.scalar_tensor_tensor(wsum[:, :, :], top[:, :, 0:1], 1e-20, top[:, :, 1:2], ALU.add, ALU.add)\
                   .then_inc(g_step, 1)
                dve.wait_ge(g_step, START + at + 4)
                dve.tensor_copy(topf[:, :, :], topi[:, :, 0:2])
                dve.reciprocal(wsum[:, :, :], wsum[:, :, :]).then_inc(g_step, 1)
                dve.wait_ge(g_step, START + at + 5)
                dve.scalar_tensor_tensor(topw[:, :, :], top[:, :, 0:2], ROUTE, wsum[:, :, :].broadcast_to([P, NT, 2]),
                                         ALU.mult, ALU.mult).then_inc(g_step, 1)
                dve.wait_ge(g_step, START + at + 6)
                for k in range(2):
                    for t in range(NT):
                        last = dve.tensor_scalar(comb[:, k, t, :], iota_sb[:, :], topf[:, t, k:k + 1],
                                                 topw[:, t, k:k + 1], ALU.is_equal, ALU.mult)
                last.then_inc(g_step, 1)
                dve.wait_ge(g_step, START + at + 7)
                dve.tensor_tensor(comb_f[:, :, :], comb[:, 0], comb[:, 1], ALU.add).then_inc(g_step, 1)
                dve.wait_ge(g_step, START + at + 8)
                split(comb_f, comb_r, comb_part, g_step, at + 8)

            def expert(b, c):
                n = 14 * b + 3 * c
                dve.wait_ge(tanh_done, START + FC * b + c + 1)
                dve.scalar_tensor_tensor(ga[:, c % 2, :], th[:, c % 2, :], 1.0, c_bank[0][:, :],
                                         ALU.add, ALU.mult).then_inc(gate_done, 1)
                dve.wait_ge(c_ready, START + 44 * b + 36 + 2 * c)
                dve.wait_ge(gate_done, START + n + 1)
                dve.scalar_tensor_tensor(hm[:, c, :], ga[:, c % 2, :], 0.5, c_bank[1][:, :],
                                         ALU.mult, ALU.mult).then_inc(gate_done, 1)
                if c < FC - 1:
                    dve.wait_ge(xb_ready, START + 9 * b + 6 + c)
                    dve.wait_ge(gate_done, START + n + 2)
                    dve.tensor_tensor(hm[:, c, :], hm[:, c, :], x_bank[:, :], ALU.mult)\
                       .then_inc(gate_done, 1)

            def result(b):
                dve.wait_ge(down_done, START + b + 1)
                dve.wait_ge(y_out, START + 16 * b)
                dve.tensor_tensor(yo[:, :, :], x_bank[:, :].rearrange("p (t d) -> p t d", d=P), x2[:, :, :],
                                  ALU.add).then_inc(y_ready, 1)

            def c_slot(b, i):
                if i == 0:
                    c_stats(b)
                elif i == 1:
                    c_keys(b)
                    c_apply(b)
                    c_front(b)
                elif i == 3:
                    c_max(b)
                elif i == 9:
                    c_tail(b)
                elif i == 10:
                    norm_apply(x2, mvx, rstdx, xn2, x_ln, 6 * b + 3, x_rstd, 4 * b + 4)
                    routing(b)
                elif i in EXPERT_SLOTS:
                    for c in EXPERT_SLOTS[i]:
                        expert(b, c)
                if i == SLOTS - 1:
                    result(b)

            def step(b, cb, last=False):
                for grp in range(4):
                    for k in range(3):
                        i = 3 * grp + k
                        if not (last and grp == 3):
                            part = max_part(grp, k, last)
                            if i == 3 and not last:
                                s_apply(b + 1)
                            s_max(b + (grp == 3), (grp + 1) % 4, part, last)
                        s_decay(b, i)
                        if not last:
                            if i == 2:
                                s_stats(b + 1)
                            elif i == 3:
                                s_front(b + 1)
                        if cb is not None:
                            c_slot(cb, i)
                s_tail(b, 0)
                s_tail(b, 1)
                if cb is not None:
                    c_slot(cb, 12)
                s_result(b)
                for i in range(13, SLOTS):
                    if cb is not None:
                        c_slot(cb, i)

            s_stats(0)
            s_apply(0)
            s_front(0)
            s_max(0, 0, range(NM), False)
            step(0, None)
            with dve.Fori(1, B - 1) as b:
                step(b, b - 1)
            step(B - 1, B - 2, last=True)
            for i in range(SLOTS):
                c_slot(B - 1, i)

        @block.tensor
        def _(pe):
            def mm(dst, lhsT, rhs, start=True, stop=True):
                return pe.matmul(dst, lhsT, rhs, start=start, stop=stop, skip_group_check=True)

            def s_front(b, part):
                n = front_uses(b)
                if part == 0:
                    pe.wait_ge(s_ln, START + 3 * b + 3)
                    pe.wait_ge(mb_free[0], START + n)
                    for t in range(NT):
                        last = pe.transpose(mx_bank[0][:, P * t:P * t + P], xn[:, t, :], id_f[:, :])
                    last.then_inc(s_tr, 1)
                    return
                pe.wait_ge(mb_free[0], START + n + 1)
                pe.wait_ge(mb_free[1], START + n)
                mm(mx_bank[1][:, :], w_sb[:, WQ, :], xnT[:, :]).then_inc(s_proj, 1)
                mm(mx_bank[0][:, :], w_sb[:, WK, :], xnT[:, :]).then_inc(s_proj, 1)
                pe.wait_ge(mb_free[1], START + n + 1)
                for t in range(NT):
                    last = mm(mx_bank[1][:, P * t:P * t + P], xnT[:, P * t:P * t + P], w_sb[:, WV, :])
                last.then_inc(s_proj, 1)

            def s_max(b, grp, part, last):
                half, e = GROUPS[grp]
                base = max_uses(b, grp, last)
                for n in part:
                    qt, g0, k = MAX_TILES[n]
                    w = P * (qt + 1)
                    if n == 0:
                        pe.wait_ge(stack_in[half], START + 288 * b + 288)
                    pe.wait_ge(mb_free[n % 2], START + base + n // 2)
                    for i in range(k):
                        h = head(half, e, g0 + i)
                        mm(mx_bank[n % 2][:, w * i:w * i + w], Qs[0:KM, h, P * qt:P * qt + P],
                           Ks[0:KM, h, 0:w], stop=False)
                        ins = mm(mx_bank[n % 2][:, w * i + w - P:w * i + w], id_b[:, :], diag_b[:, :],
                                 start=False)
                    ins.then_inc(max_ready, 1)

            def s_max_turn(b, grp, last):
                pe.wait_ge(mx_split, START + 16 * b + 4 * grp + 4)
                pe.wait_ge(mb_free[1], START + max_uses(b, grp, last) + NM // 2)
                for t in range(NT):
                    ins = pe.transpose(mx_bank[1][:, P // 2 * t:P // 2 * (t + 1)].bitcast(BF16),
                                       mx_part[:, t].rearrange("p i h -> p (i h)"), id_b[:, :])
                ins.then_inc(mx_tr, 1)

            def s_scores(b, t):
                half, e = GROUPS[t // TPG]
                if t % TPG == 0:
                    pe.wait_ge(max_row, START + 128 * b + 32 * (t // TPG) + 32)
                if t >= 2:
                    pe.wait_ge(exp_done, START + TILES * b + t - 1)
                else:
                    pe.wait_ge(exp_done, START + TILES * b)
                for g, kt, c in PIECES[t % TPG]:
                    h = head(half, e, g)
                    w = N - P * kt
                    last = mm(sc_bank[t % 2][:, c:c + w], Ks[0:KS, h, P * kt:P * kt + P],
                              Qs[0:KS, h, P * kt:N])
                last.then_inc(sc_ready, 1)

            def s_values(b, s):
                half, e = GROUPS[s // 3]
                if s % 6 == 0:
                    pe.wait_ge(v_in, START + b + 1)
                    pe.wait_ge(sb_free, START + 6 * b + s // 6)
                t1 = TPG * (s // 3) + SETS[s % 3][1] - 1
                pe.wait_ge(dec_dve, START + DVE_N * b + applied_before(t1, False))
                pe.wait_ge(dec_pool, START + POOL_N * b + applied_before(t1, True))
                pieces = [(i, *piece) for i in range(*SETS[s % 3]) for piece in PIECES[i]]
                for i, g, kt, c in sorted(pieces, key=lambda p: (p[2], p[1])):
                    h = head(half, e, g)
                    w = N - P * kt
                    last = mm(s_bank[32 * g:32 * g + 32, P * kt:N], Vs[:, kt, h, :], Ps[:, i, c:c + w],
                              start=(e == 0 and kt == 0), stop=(e == 1 and kt == 2))
                last.then_inc(pv_done, 1)

            def s_tail(b, part):
                if part < 2:
                    pe.wait_ge(sb_free, START + 6 * b + 2 + part)
                    for t in range(NT):
                        last = pe.transpose(s_bank[:, P * t:P * t + P], Nh[:, part, P * t:P * t + P], id_f[:, :])
                elif part == 2:
                    pe.wait_ge(sb_free, START + 6 * b + 4)
                    for t in range(NT):
                        last = pe.transpose(s_bank[:, P * t:P * t + P], at[:, t, :], id_f[:, :])
                else:
                    pe.wait_ge(sb_free, START + 6 * b + 5)
                    for t in range(NT):
                        last = mm(s_bank[:, P * t:P * t + P], atT[:, P * t:P * t + P], w_sb[:, WO, :])
                last.then_inc(n_tr, 1)

            def c_use(b, u):
                pe.wait_ge(c_free[u % 2], START + 17 * b + u // 2)
                return c_bank[u % 2]

            def c_keys(b):
                pe.wait_ge(gate_done, START + 14 * b)
                ps = c_use(b, 0)
                pe.wait_ge(ctx_in_s, START + 16 * b + 16)
                pe.transpose(ps[:, 0:NK], cin[:, :], id_f[0:NK, 0:NK]).then_inc(c_ready, 1)
                pe.wait_ge(c_free[0], START + 17 * b + 1)
                ps = c_use(b, 1)
                mm(ps[:, 0:NK], w_sb[:, WXK, :], cT[:, :]).then_inc(c_ready, 1)
                ps = c_use(b, 2)
                mm(ps[0:NK, 0:P], cT[:, :], w_sb[:, WXV, :]).then_inc(c_ready, 1)

            def c_front(b):
                pe.wait_ge(x_ln, START + 6 * b + 3)
                ps = c_use(b, 3)
                for t in range(NT):
                    last = pe.transpose(ps[:, P * t:P * t + P], xn2[:, t, :], id_f[:, :])
                last.then_inc(c_ready, 1)
                pe.wait_ge(c_free[1], START + 17 * b + 2)
                ps = c_use(b, 4)
                mm(ps[:, :], w_sb[:, WXQ, :], xn2T[:, :]).then_inc(c_ready, 1)

            def c_max(b):
                pe.wait_ge(xk_in, START + 144 * b + 144)
                pe.wait_ge(mask_rows, START + 48 * b + 48)
                pe.wait_ge(xq_in, START + 144 * b + 144)
                for n, (qt, h0, k) in enumerate(XMAX_TILES):
                    ps = c_use(b, 5 + n)
                    for i in range(k):
                        last = mm(ps[:, NK * i:NK * i + NK], Qx[0:KMX, h0 + i, P * qt:P * qt + P],
                                  Kx[0:KMX, h0 + i, 0:NK])
                    last.then_inc(c_ready, 1)

            def c_max_turn(b):
                pe.wait_ge(xmx_split, START + 4 * b + 4)
                pe.wait_ge(y_ready, START + b)
                for t in range(NT):
                    last = pe.transpose(x_bank[:, P // 2 * t:P // 2 * (t + 1)].bitcast(BF16),
                                        mxx_part[:, t].rearrange("p i h -> p (i h)"), id_b[:, :])
                last.then_inc(xb_ready, 1)

            def c_scores(b, s):
                if s == 0:
                    pe.wait_ge(xmax_row, START + 32 * b + 32)
                for g in range(4):
                    h = head(s // 2, s % 2, g)
                    ps = c_use(b, 17 + 4 * s + g)
                    mm(ps[:, :], Kx[0:KSX, h, :], Qx[0:KSX, h, :]).then_inc(c_ready, 1)

            def c_values(b, v):
                pe.wait_ge(c_free[0], START + 17 * b + 11 + 2 * v)
                pe.wait_ge(c_free[1], START + 17 * b + 10 + 2 * v)
                if v % 2 == 0:
                    pe.wait_ge(xb_free, START + 7 * b + 1 + v // 2)
                for g in range(4):
                    last = mm(x_bank[32 * g:32 * g + 32, :], Vx[:, head(v // 2, v % 2, g), :],
                              Px[:, 4 * (v % 2) + g, :], start=v % 2 == 0, stop=v % 2 == 1)
                last.then_inc(xpv_done, 1)

            def c_tail(b):
                for half in range(2):
                    pe.wait_ge(xb_free, START + 7 * b + 3 + half)
                    for t in range(NT):
                        last = pe.transpose(x_bank[:, P * t:P * t + P], Nx[:, half, P * t:P * t + P], id_f[:, :])
                    last.then_inc(xb_ready, 1)

            def experts_in(b):
                pe.wait_ge(x_ln, START + 6 * b + 6)
                ps = c_use(b, 33)
                for t in range(NT):
                    last = pe.transpose(ps[:, P * t:P * t + P], xn2[:, t, :], id_f[:, :])
                last.then_inc(c_ready, 1)
                pe.wait_ge(c_free[1], START + 17 * b + 17)
                pe.wait_ge(xb_free, START + 7 * b + 5)
                for t in range(NT):
                    last = mm(x_bank[:, E * t:E * t + E], xn2T[:, P * t:P * t + P], gate_sb[:, :])
                last.then_inc(xb_ready, 1)

            def expert(b, c):
                for k, w in enumerate((wg_sb, wu_sb)):
                    if c:
                        pe.wait_ge(gate_done, START + 14 * b + 3 * (c - 1) + 1 + k)
                    else:
                        pe.wait_ge(c_free[k], START + 17 * b + 17)
                    mm(c_bank[k][:, :], w[:, P * c:P * c + P], xn2T[:, :]).then_inc(c_ready, 1)
                if c == 0:
                    pe.wait_ge(g_step, START + 12 * b + 12)
                    pe.wait_ge(xb_free, START + 7 * b + 6)
                    for t in range(NT):
                        last = pe.transpose(x_bank[:, P // 2 * t:P // 2 * (t + 1)].bitcast(BF16),
                                            comb_part[:, t].rearrange("p i e -> p (i e)"), id_b[:, :])
                    last.then_inc(xb_ready, 1)
                if c < FC - 1:
                    if c:
                        pe.wait_ge(gate_done, START + 14 * b + 3 * c)
                    else:
                        pe.wait_ge(xb_free, START + 7 * b + 7)
                    mm(x_bank[:, :], sel_b[:, c, :], combT[:, :]).then_inc(xb_ready, 1)

            def experts_out(b):
                pe.wait_ge(gate_done, START + 14 * b + 14)
                for t in range(NT):
                    for c in range(FC):
                        last = mm(x_bank[:, P * t:P * t + P], hm[:, c, P * t:P * t + P], wd_sb[:, c, :],
                                  start=c == 0, stop=c == FC - 1)
                last.then_inc(down_done, 1)

            pe.wait_ge(w_in, 16 * N_W)
            pe.wait_ge(mask_in, 48)
            pe.wait_ge(preset, 3)
            pe.wait_ge(set_up, 1)

            def c_slot(b, i):
                if i == 1:
                    c_keys(b)
                    c_front(b)
                elif i == 3:
                    c_max(b)
                elif i == 4:
                    c_max_turn(b)
                elif 5 <= i < 9:
                    c_scores(b, i - 5)
                if 6 <= i < 10:
                    c_values(b, i - 6)
                if i == 9:
                    c_tail(b)
                elif i == 10:
                    experts_in(b)
                elif i in EXPERT_SLOTS:
                    for c in EXPERT_SLOTS[i]:
                        expert(b, c)
                if i == SLOTS - 1:
                    experts_out(b)

            def step(b, cb, last=False):
                for grp in range(4):
                    for k in range(3):
                        i = 3 * grp + k
                        if not (last and grp == 3):
                            if k == 2:
                                s_max_turn(b + (grp == 3), (grp + 1) % 4, last)
                            if i == 3 and not last:
                                s_front(b + 1, 0)
                            s_max(b + (grp == 3), (grp + 1) % 4, max_part(grp, k, last), last)
                        for t in set_tiles(i):
                            s_scores(b, t)
                        if i:
                            s_values(b, i - 1)
                        if i == 3 and not last:
                            s_front(b + 1, 1)
                        if cb is not None:
                            c_slot(cb, i)
                s_values(b, 11)
                for part in range(3):
                    s_tail(b, part)
                if cb is not None:
                    c_slot(cb, 12)
                s_tail(b, 3)
                for i in range(13, SLOTS):
                    if cb is not None:
                        c_slot(cb, i)

            s_front(0, 0)
            s_front(0, 1)
            s_max(0, 0, range(NM), False)
            s_max_turn(0, 0, False)
            step(0, None)
            with pe.Fori(1, B - 1) as b:
                step(b, b - 1)
            step(B - 1, B - 2, last=True)
            for i in range(SLOTS):
                c_slot(B - 1, i)


def kernel(**inputs):
    import numpy as np
    import concourse.bacc as bacc
    from concourse.bass_utils import run_bass_kernel_spmd as run

    a = {k: np.ascontiguousarray(v) for k, v in inputs.items()}
    i, j = np.arange(P)[:, None], np.arange(P)[None, :]
    delta = np.arange(N)[None, :] - np.arange(P)[:, None]
    part_expert = np.arange(P)[:, None, None]
    column_expert = 2 * np.arange(4)[None, :, None] + np.arange(P)[None, None, :] // 64
    ffn = "L0_ffn_"
    arrays = {
        "x": a["x"], "ctx_in": a["ctx_1024"], "mask": a["mask_BxS2_ik0"],
        "wq": a["L0_attn_Wq"], "wk": a["L0_attn_Wk"], "wv": a["L0_attn_Wv"], "wo": a["L0_attn_Wo"],
        "wxq": a["L0_xattn_Wq"].T, "wxk": a["L0_xattn_Wk"].T, "wxv": a["L0_xattn_Wv"].T,
        "bias_cols": np.stack([a["L0_attn_bq"], a["L0_attn_bk"], a["L0_xattn_bq"], a["L0_xattn_bk"]]),
        "bias_rows": np.stack([a["L0_attn_bv"], a["L0_attn_bo"], a["L0_xattn_bv"]]),
        "wg": np.concatenate([a[ffn + "w_gate"].reshape(512, P), a[ffn + "ws_gate"]]).T,
        "wu": np.concatenate([a[ffn + "w_up"].reshape(512, P), a[ffn + "ws_up"]]).T,
        "wd": np.concatenate([a[ffn + "w_down"].transpose(0, 2, 1).reshape(4, P, P), a[ffn + "ws_down"].T[None]]),
        "gate": a[ffn + "gate_weight"].T,
        "ident": np.eye(P, dtype=np.float32),
        "diag": np.where(j > i, np.float32(FAR), np.float32(0)).astype(np.float32),
        "decay": np.where(delta < 0, 0.0, np.maximum(delta, 1).astype(np.float64) ** -0.25).astype(np.float32),
        "sel": np.where(part_expert < NPART * E, part_expert % E == column_expert, False).astype(np.float32),
        "iota": np.tile(np.arange(E, dtype=np.float32), (P, 1)),
    }
    arrays = {k: np.ascontiguousarray(v) for k, v in arrays.items()}
    nc = bacc.Bacc("TRN2", target_bir_lowering=False, num_devices=1)
    args = {k: nc.dram_tensor(k, v.shape, mybir.dt.from_np(v.dtype), kind="ExternalInput").ap()
            for k, v in arrays.items()}
    out = nc.dram_tensor("out", (B, N, P), F32, kind="ExternalOutput").ap()
    decoder_layer(nc, out=out, **args)
    return run(nc, [arrays], core_ids=[0]).results[0]["out"]
```

```python
import struct
from contextlib import ExitStack

import concourse.bass as bass
from concourse import mybir

ALU = mybir.AluOpType
ACT = mybir.ActivationFunctionType
AX_X = mybir.AxisListType.X
F32 = mybir.dt.float32
BF16 = mybir.dt.bfloat16
I32 = mybir.dt.int32
U32 = mybir.dt.uint32

P = 128
B = 4
N = 512
NT = N // P
H = 16
DK = P // H
NK = 77
E = 8
FC = 5
NPART = 3
QK = NPART * NPART * DK
ROWX = 96
KM = 96
KS = ROWX + NPART
KMX = ROWX + NPART
KSX = ROWX + 2 * NPART
SCALE = float(DK) ** -0.5
EPS = 1e-5
ROUTE = 2.5
TWO_ONES = struct.unpack("f", struct.pack("I", 0x3F803F80))[0]
START = 1
FAR = -1e30

MAX_TILES = [(qt, g, k) for qt, k in enumerate((4, 2, 1, 1)) for g in range(0, 4, k)]
NM = len(MAX_TILES)
XMAX_TILES = [(qt, h, n) for qt in range(NT) for h, n in ((0, 6), (6, 5), (11, 5))]
PIECES = ([[(g, 0, 0)] for g in range(4)]
          + [[(g, 1, 0), (g, 3, 384)] for g in range(4)]
          + [[(0, 2, 0), (1, 2, 256)], [(2, 2, 0), (3, 2, 256)]])
SETS = [(0, 4), (4, 8), (8, 10)]
GROUPS = [(half, e) for half in range(2) for e in range(2)]
SLOTS = 3 * len(GROUPS)
STEPS = 4
HEAD = SLOTS // 3
X_MAX = {(4, 3): (0, 1), (5, 1): (2, 3), (5, 2): (4, 5), (5, 3): (6, 7), (6, 0): (8, 9), (6, 1): (10, 11)}
X_SCORES = {(7, 2): (0,), (7, 3): (1,), (8, 0): (2, 3), (8, 1): (4, 5), (8, 2): (6, 7), (8, 3): (8, 9),
            (9, 0): (10,), (9, 1): (11,), (9, 2): (12,), (9, 3): (13,), (10, 0): (14,), (10, 1): (15,)}
X_VALUES = {(8, 2): 0, (9, 0): 1, (9, 3): 2, (10, 3): 3}
TPG = len(PIECES)
TILES = TPG * len(GROUPS)
POOL_TILES = (0, 3, 5, 8)


def heads(half, e):
    return slice(8 * half + e, 8 * half + 8, 2)


def head(half, e, g):
    return 8 * half + 2 * g + e


def on_pool(t):
    return t % TPG in POOL_TILES


def set_tiles(s):
    return range(TPG * (s // 3) + SETS[s % 3][0], TPG * (s // 3) + SETS[s % 3][1])


def applied_before(t, pool):
    return sum(on_pool(x) == pool for x in range(t + 1))


def kind_of(t):
    return 0 if t % TPG < 4 else 1 if t % TPG < 8 else 2


def first(b):
    return isinstance(b, int) and b == 0


BANK_USES = (4 + 4 * (NM + 1)) // 2


def front_uses(b):
    return 0 if first(b) else BANK_USES * b - 6


def max_uses(b, grp, last=False):
    if grp == 0:
        return BANK_USES * b + 2
    return BANK_USES * b + 8 + 6 * (grp - 1) + (2 if grp == 3 and not last else 0)


C_USES = 36
CT, KV, AT, OUT_PROJ, XNT, XQ, XMAX, XSCORE = 1, 2, 4, 5, 6, 7, 8, 20
HALF = (0, 3)
BETWEEN = (4, 6, 6, 7, 7)


def pairs_before(b, u):
    return 0 if first(b) else sum(n <= u for n in BETWEEN)


def c_uses(b, u):
    return (0 if first(b) else (C_USES // 2 + FC) * b - FC) + u // 2 + pairs_before(b, u)


def c_written(b, u):
    return (0 if first(b) else (C_USES + 2 * FC) * b - 2 * FC) + u + 2 * pairs_before(b, u) + 1


def between(b, c):
    return 0 if isinstance(b, int) and b == B - 1 else BETWEEN[c]


def e_uses(b, c, k):
    return (C_USES // 2 + FC) * (b + 1) - FC + (between(b, c) + 1 - k) // 2 + c


def e_written(b, c, k):
    return (C_USES + 2 * FC) * (b + 1) - 2 * FC + between(b, c) + 2 * c + k + 1


def s_tiles(i, j):
    tiles = set_tiles(i)
    return tiles[j:j + 1] if i % 3 < 2 else tiles if j == 0 else ()


def maxima(i, j):
    if i % 3 < 2:
        return (3 + 4 * (i % 3) + j,)
    if i == 5:
        return range(3) if j == 3 else ()
    return (j - 1,) if j else ()


def max_group(s, i):
    grp = i // 3 + 1 + (i % 3 == 2)
    return s + grp // 4, grp % 4


def max_stage(i, last):
    return not (last and i >= SLOTS - 4)


def batches(engine, slot):
    def body(b, last=False):
        for i in range(HEAD, SLOTS):
            slot(i, s=b, c=None if first(b) else b - 1, last=last)
        for i in range(HEAD):
            slot(i, s=None if last else b + 1, c=b, e=None if first(b) else b - 1)

    for i in range(HEAD):
        slot(i, s=0)
    body(0)
    with engine.Fori(1, B - 1) as b:
        body(b)
    body(B - 1, last=True)
    for i in range(HEAD, SLOTS):
        slot(i, c=B - 1)
    for i in range(HEAD):
        slot(i, e=B - 1)


POOL_N, DVE_N = applied_before(TILES - 1, True), applied_before(TILES - 1, False)


def decoder_layer(nc, x, ctx_in, mask, wq, wk, wv, wo, wxq, wxk, wxv, bias_cols, bias_rows,
                  wg, wu, wd, gate, ident, diag, decay, sel, iota, out):
    x_v = x.rearrange("b (t p) d -> b p t d", p=P)
    out_v = out.rearrange("b (t p) d -> b p t d", p=P)

    ctx = ExitStack()
    with ctx:
        def sb(name, shape, dt=F32):
            return ctx.enter_context(nc.sbuf_tensor(name, shape, dt))

        def sem(name):
            s = ctx.enter_context(nc.semaphore(name))
            counted.append(s)
            return s

        counted = []

        q_scr = nc.dram_tensor("q_scr", (NPART, P, N), BF16, kind="Internal").ap()
        k_scr = nc.dram_tensor("k_scr", (2 * NPART - 1, P, N), BF16, kind="Internal").ap()
        qx_scr = nc.dram_tensor("qx_scr", (NPART, P, N), BF16, kind="Internal").ap()
        mask_scr = nc.dram_tensor("mask_scr", (NPART, B, P), BF16, kind="Internal").ap()
        mx_scr = nc.dram_tensor("mx_scr", (NPART * 4, N), BF16, kind="Internal").ap()
        mxx_scr = nc.dram_tensor("mxx_scr", (NPART * H, N), BF16, kind="Internal").ap()
        kx_scr = nc.dram_tensor("kx_scr", (2 * NPART - 1, P, NK), BF16, kind="Internal").ap()

        w_sb = sb("w_sb", [P, 7, P])
        WQ, WK, WV, WO, WXQ, WXK, WXV = range(7)
        bcol = sb("bcol", [P, 4])
        brow = sb("brow", [P, 3, P])
        wg_sb = sb("wg_sb", [P, FC * P])
        wu_sb = sb("wu_sb", [P, FC * P])
        wd_sb = sb("wd_sb", [P, FC, P])
        gate_sb = sb("gate_sb", [P, E])
        id_f = sb("id_f", [P, P])
        id_b = sb("id_b", [P, P], BF16)
        diag_f = sb("diag_f", [P, P])
        diag_b = sb("diag_b", [P, P], BF16)
        dec = sb("dec", [P, 3, N])
        sel_f = sb("sel_f", [P, 4, P])
        sel_b = sb("sel_b", [P, 4, P], BF16)
        iota_sb = sb("iota_sb", [P, E])
        spare = sb("spare", [P, 4])
        half_pow = sb("half_pow", [P, NT])
        eps_sb = sb("eps_sb", [P, NT])
        mask_i = sb("mask_i", [B, NK], I32)
        mask_s = sb("mask_s", [B, 2, P])
        mask_b = sb("mask_b", [B, NPART, P], BF16)

        xin = sb("xin", [P, NT, P])
        xb = sb("xb", [P, NT, P])
        stats = sb("stats", [P, NT, 6])
        mv = sb("mv", [P, NT, 2])
        ve = sb("ve", [P, NT])
        rstd = sb("rstd", [P, NT])
        xn = sb("xn", [P, NT, P])
        xnT = sb("xnT", [P, N])
        qk_f = sb("qk_f", [P, 2, N])
        qk_r = sb("qk_r", [P, 2, N])
        q_part = sb("q_part", [P, NPART, N], BF16)
        k_part = sb("k_part", [P, NPART, N], BF16)
        Qs = sb("Qs", [P, H, N], BF16)
        Ks = sb("Ks", [P, H, N], BF16)
        Vs = sb("Vs", [P, NT, H, 32])
        v_sb = sb("v_sb", [P, NT, P])
        mx = sb("mx", [P, NT, 4])
        mx_r = sb("mx_r", [P, NT, 4])
        mx_part = sb("mx_part", [P, NT, P // 4, 4], BF16)
        mxT = sb("mxT", [NPART * 4, N], BF16)
        Ps = sb("Ps", [P, TPG, N])
        Nh = sb("Nh", [P, 2, N])
        den = sb("den", [P, NT * 4, 2])
        at = sb("at", [P, NT, P])
        atT = sb("atT", [P, N])
        x1 = sb("x1", [P, NT, P])

        cin = sb("cin", [NK, P])
        cT = sb("cT", [P, NK])
        kx_f = sb("kx_f", [P, NK])
        kx_r = sb("kx_r", [P, NK])
        kx_part = sb("kx_part", [P, NPART, NK], BF16)
        Kx = sb("Kx", [P, H, P], BF16)
        Vx = sb("Vx", [P, H, 32])
        statsx = sb("statsx", [P, NT, 6])
        mvx = sb("mvx", [P, NT, 2])
        vex = sb("vex", [P, NT])
        rstdx = sb("rstdx", [P, NT])
        xn2 = sb("xn2", [P, NT, P])
        xn2T = sb("xn2T", [P, N])
        qx_f = sb("qx_f", [P, N])
        qx_r = sb("qx_r", [P, N])
        qx_part = sb("qx_part", [P, NPART, N], BF16)
        Qx = sb("Qx", [P, H, N], BF16)
        mxx = sb("mxx", [P, NT, H])
        mxx_r = sb("mxx_r", [P, NT, H])
        mxx_part = sb("mxx_part", [P, NT, P // H, H], BF16)
        mxxT = sb("mxxT", [NPART * H, N], BF16)
        Px = sb("Px", [P, 8, N])
        Nx = sb("Nx", [P, 2, N])
        denx = sb("denx", [P, NT * 4, 2])
        atx = sb("atx", [P, NT, P])
        x2 = sb("x2", [P, NT, P])
        eg = sb("eg", [P, NT, E])
        sg = sb("sg", [P, NT, E])
        top = sb("top", [P, NT, 8])
        topi = sb("topi", [P, NT, 8], U32)
        topf = sb("topf", [P, NT, 2])
        wsum = sb("wsum", [P, NT, 1])
        topw = sb("topw", [P, NT, 2])
        comb = sb("comb", [P, 2, NT, E])
        comb_f = sb("comb_f", [P, NT, E])
        comb_r = sb("comb_r", [P, NT, E])
        comb_part = sb("comb_part", [P, NT, P // E, E], BF16)
        combT = sb("combT", [P, N], BF16)
        xe = sb("xe", [P, NT, P])
        xeT = sb("xeT", [P, N])
        th = sb("th", [P, N])
        ga = sb("ga", [P, N])
        hm = sb("hm", [P, FC, N])
        yo = sb("yo", [P, NT, P])

        bank = [ctx.enter_context(nc.psum_tensor(f"bank{i}", [P, N], F32)) for i in range(8)]
        sc_bank = bank[0:2]
        mx_bank = bank[2:4]
        s_bank = bank[4]
        c_bank = bank[5:7]
        x_bank = bank[7]

        w_in = sem("w_in")
        mask_in = sem("mask_in")
        set_up = sem("set_up")
        mask_ready = sem("mask_ready")
        mask_out = sem("mask_out")
        preset = sem("preset")

        counted.clear()
        x_in = sem("x_in")
        s_ln = sem("s_ln")
        s_rstd = sem("s_rstd")
        xb_done = sem("xb_done")
        v_in = sem("v_in")
        s_tr = sem("s_tr")
        s_proj = sem("s_proj")
        s_split = sem("s_split")
        scr_out = sem("scr_out")
        stack_in = [sem("stack_in0"), sem("stack_in1")]
        max_ready = sem("max_ready")
        mb_free = [sem("mb_free0"), sem("mb_free1")]
        mx_split = sem("mx_split")
        mx_tr = sem("mx_tr")
        max_row = sem("max_row")
        sc_ready = sem("sc_ready")
        exp_done = sem("exp_done")
        dec_dve = sem("dec_dve")
        dec_pool = sem("dec_pool")
        pv_done = sem("pv_done")
        sb_free = sem("sb_free")
        s_norm = sem("s_norm")

        mask_rows = sem("mask_rows")
        ctx_in_s = sem("ctx_in_s")
        x_ln = sem("x_ln")
        x_rstd = sem("x_rstd")
        c_ready = sem("c_ready")
        c_free = [sem("c_free0"), sem("c_free1")]
        x_split = sem("x_split")
        kx_ready = sem("kx_ready")
        xscr_out = sem("xscr_out")
        xk_in = sem("xk_in")
        xq_in = sem("xq_in")
        xmx_split = sem("xmx_split")
        xmax_row = sem("xmax_row")
        xpv_done = sem("xpv_done")
        xb_ready = sem("xb_ready")
        xb_free = sem("xb_free")
        x_norm = sem("x_norm")
        g_sig = sem("g_sig")
        g_step = sem("g_step")
        tanh_done = sem("tanh_done")
        gate_done = sem("gate_done")
        down_done = sem("down_done")
        y_ready = sem("y_ready")
        y_out = sem("y_out")

        with nc.Block() as start:
            @start.sync
            def _(sp):
                for s in counted:
                    sp.sem_inc(s, START)

        N_W = 7 + 4 + 3 + 11
        block = ctx.enter_context(nc.Block())

        @block.sync
        def _(sp):
            sp.dma_start(mask_i[:, :], mask).then_inc(mask_in, 16)
            for i, w in enumerate((wq, wk, wv, wo, wxq, wxk, wxv)):
                sp.dma_start(w_sb[:, i, :], w).then_inc(w_in, 16)
            for i in range(4):
                sp.dma_start(bcol[:, i:i + 1], bias_cols[i].rearrange("(d o) -> d o", o=1)).then_inc(w_in, 16)
            for i in range(3):
                sp.dma_start(brow[:, i, :], bias_rows[i].partition_broadcast(P)).then_inc(w_in, 16)
            sp.dma_start(id_f[:, :], ident).then_inc(w_in, 16)
            sp.dma_start(diag_f[:, :], diag).then_inc(w_in, 16)
            sp.dma_start(dec[:, 0, :], decay).then_inc(w_in, 16)
            sp.dma_start(dec[:, 1, 0:384], decay[:, 0:384]).then_inc(w_in, 16)
            sp.dma_start(dec[:, 1, 384:512], decay[:, 0:128]).then_inc(w_in, 16)
            sp.dma_start(dec[:, 2, 0:256], decay[:, 0:256]).then_inc(w_in, 16)
            sp.dma_start(dec[:, 2, 256:512], decay[:, 0:256]).then_inc(w_in, 16)
            sp.dma_start(sel_f[:, :, :], sel).then_inc(w_in, 16)
            sp.dma_start(iota_sb[:, :], iota).then_inc(w_in, 16)
            sp.dma_start(gate_sb[:, :], gate).then_inc(w_in, 16)
            sp.dma_start(wd_sb[:, :, :], wd.rearrange("c f h -> f c h")).then_inc(w_in, 16)
            sp.dma_start(wg_sb[:, :], wg).then_inc(mask_in, 16)
            sp.dma_start(wu_sb[:, :], wu).then_inc(mask_in, 16)

            def load_x(b):
                sp.wait_ge(xb_done, START + b)
                sp.wait_ge(s_ln, START + 3 * b)
                sp.dma_start(xin[:, :, :], x_v[b]).then_inc(x_in, 16)

            def stack_rows(scr):
                return scr.rearrange("i (d h) t -> (i d) h t", h=H)

            def parts_out(b):
                sp.wait_ge(s_split, START + 6 * b + 6)
                sp.dma_start(q_scr.rearrange("i r t -> r i t"), q_part[:, :, :]).then_inc(scr_out, 16)
                sp.dma_start(k_scr[0:NPART].rearrange("i r t -> r i t"), k_part[:, :, :]).then_inc(scr_out, 16)
                sp.dma_start(k_scr[NPART:].rearrange("i r t -> r i t"), k_part[:, 0:NPART - 1, :])\
                  .then_inc(scr_out, 16)

            def stacks_in(b, half):
                if not first(b):
                    sp.wait_ge(sc_ready, START + TILES * b - TILES // 2 * (1 - half))
                sp.wait_ge(scr_out, START + 48 * b + 48)
                for s in range(NPART):
                    row = DK * NPART * s
                    for stack, scr, at in ((Qs, q_scr, 0), (Ks, k_scr, DK * s)):
                        sp.dma_start(stack[row:row + DK * NPART, 8 * half:8 * half + 8, :],
                                     stack_rows(scr)[at:at + DK * NPART, 8 * half:8 * half + 8, :])\
                          .then_inc(stack_in[half], 16)

            def s_max_rows(b, grp, last):
                sp.wait_ge(mb_free[1], START + max_uses(b, grp, last) + NM // 2 + 1)
                sp.dma_start(mx_scr, mxT[:, :]).then_inc(max_row, 16)
                sp.wait_ge(max_row, START + 128 * b + 32 * grp + 16)
                sp.dma_start(Qs[ROWX:ROWX + NPART, heads(*GROUPS[grp]), :],
                             mx_scr.rearrange("(i h) t -> i h t", h=4)).then_inc(max_row, 16)

            def load_ctx(b):
                if not first(b):
                    sp.wait_ge(c_ready, START + c_written(b - 1, XMAX))
                sp.dma_start(cin[:, :], ctx_in[b]).then_inc(ctx_in_s, 16)

            def mask_row(b):
                sp.wait_ge(xpv_done, START + 4 * b)
                for i in reversed(range(NPART)):
                    sp.dma_start(Kx[ROWX + i:ROWX + i + 1, :, :],
                                 mask_scr[i:i + 1, bass.ds(b, 1), :].broadcast_to([1, H, P]))\
                      .then_inc(mask_rows, 16)

            def x_keys(b):
                sp.wait_ge(x_split, START + 6 * b + 3)
                sp.dma_start(kx_scr[0:NPART].rearrange("i r t -> r i t"), kx_part[:, :, :]).then_inc(xscr_out, 16)
                sp.dma_start(kx_scr[NPART:].rearrange("i r t -> r i t"), kx_part[:, 0:NPART - 1, :])\
                  .then_inc(xscr_out, 16)
                sp.wait_ge(xscr_out, START + 48 * b + 32)
                for s in range(NPART):
                    row = DK * NPART * s
                    sp.dma_start(Kx[row:row + DK * NPART, :, 0:NK],
                                 stack_rows(kx_scr)[DK * s:DK * (s + NPART)]).then_inc(xk_in, 16)

            def x_queries(b):
                sp.wait_ge(x_split, START + 6 * b + 6)
                sp.dma_start(qx_scr.rearrange("i r t -> r i t"), qx_part[:, :, :]).then_inc(xscr_out, 16)
                sp.wait_ge(xscr_out, START + 48 * b + 48)
                for s in range(NPART):
                    row = DK * NPART * s
                    sp.dma_start(Qx[row:row + DK * NPART, :, :], stack_rows(qx_scr)).then_inc(xq_in, 16)

            def x_max_rows(b):
                sp.wait_ge(xb_free, START + 8 * b + 1)
                sp.dma_start(mxx_scr, mxxT[:, :]).then_inc(xmax_row, 16)
                sp.wait_ge(xmax_row, START + 32 * b + 16)
                sp.dma_start(Qx[ROWX + NPART:ROWX + 2 * NPART, :, :], mxx_scr.rearrange("(i h) t -> i h t", h=H))\
                  .then_inc(xmax_row, 16)

            def store_y(b):
                sp.wait_ge(y_ready, START + b + 1)
                sp.dma_start(out_v[b], yo[:, :, :]).then_inc(y_out, 16)

            sp.wait_ge(preset, 1)
            sp.wait_ge(mask_ready, 6)
            sp.dma_start(mask_scr.rearrange("i b k -> b i k"), mask_b[:, :, :]).then_inc(mask_out, 16)
            sp.wait_ge(mask_out, 16)

            def slot(i, s=None, c=None, e=None, last=False):
                if s is not None:
                    if i % 3 == 2 and not (last and i == 11):
                        s_max_rows(s + (i == 11), (i // 3 + 1) % 4, last)
                    if not last:
                        if i == 4:
                            load_x(s + 1)
                        elif i == 6:
                            parts_out(s + 1)
                    if i == 10:
                        load_ctx(s)
                        mask_row(s)
                    elif i == 0 and not first(s):
                        stacks_in(s, 1)
                if c is not None:
                    if i == 1:
                        x_keys(c)
                    elif i == 3:
                        x_queries(c)
                    elif i == 6:
                        x_max_rows(c)
                if s is not None and not last and i == 6:
                    stacks_in(s + 1, 0)
                if e is not None and i == HEAD - 1:
                    store_y(e)

            load_x(0)
            parts_out(0)
            stacks_in(0, 0)
            stacks_in(0, 1)
            s_max_rows(0, 0, False)
            batches(sp, slot)
            sp.wait_ge(y_out, START + 16 * B)

        @block.gpsimd
        def _(pool):
            for stack in (Qs, Ks, Qx, Kx):
                pool.memset(stack[0:ROWX, :, :].bitcast(F32), 0.0)
            pool.memset(Vs[:, :, :, :], 0.0)
            pool.memset(Vx[:, :, :], 0.0)
            pool.memset(combT[:, :], 0.0)
            for part in (mx_part, mxx_part, comb_part):
                pool.memset(part[:, :, :, :], 0.0)
            pool.memset(eps_sb[:, :], EPS)
            pool.memset(half_pow[:, :], -0.5).then_inc(preset, 1)
            pool.wait_ge(preset, 1)
            for e in range(2):
                pool.memset(Vs[:, :, e:H:2, 16 + 8 * e:24 + 8 * e], 1.0)
                pool.memset(Vx[:, e:H:2, 16 + 8 * e:24 + 8 * e], 1.0).then_inc(preset, 1)
            pool.wait_ge(w_in, 16 * N_W)
            pool.wait_ge(preset, 3)

            def s_norm_step(b):
                pool.wait_ge(s_ln, START + 3 * b + 2)
                pool.tensor_tensor(ve[:, :], mv[:, :, 1], eps_sb[:, :], ALU.add).then_inc(s_rstd, 1)
                pool.wait_ge(s_rstd, START + 2 * b + 1)
                pool.tensor_tensor(rstd[:, :], ve[:, :], half_pow[:, :], ALU.pow).then_inc(s_rstd, 1)

            def s_bias(b):
                if not first(b):
                    pool.wait_ge(c_free[OUT_PROJ % 2], START + c_uses(b - 1, OUT_PROJ) + 1)
                pool.wait_ge(x_in, START + 16 * b + 16)
                pool.tensor_tensor(xb[:, :, :], xin[:, :, :], brow[:, 1:2, :].broadcast_to([P, NT, P]),
                                   ALU.add).then_inc(xb_done, 1)

            def s_values_in(b):
                pool.wait_ge(mb_free[1], START + front_uses(b) + 2)
                pool.wait_ge(pv_done, START + 12 * b)
                for e in range(2):
                    for t in range(NT):
                        v = v_sb[:, t].rearrange("p (g e d) -> p g e d", e=2, d=DK)[:, :, e, :]
                        bv = brow[:, 0].rearrange("p (g e d) -> p g e d", e=2, d=DK)[:, :, e, :]
                        last = pool.tensor_tensor(Vs[:, t, e:H:2, DK * e:DK * e + DK], v, bv, ALU.add)
                last.then_inc(v_in, 1)

            def x_norm_step(b, k):
                pool.wait_ge(x_ln, START + 6 * b + 3 * k + 2)
                pool.tensor_tensor(vex[:, :], mvx[:, :, 1], eps_sb[:, :], ALU.add).then_inc(x_rstd, 1)
                pool.wait_ge(x_rstd, START + 4 * b + 2 * k + 1)
                pool.tensor_tensor(rstdx[:, :], vex[:, :], half_pow[:, :], ALU.pow).then_inc(x_rstd, 1)

            def decay_tiles(b, s):
                for t in set_tiles(s):
                    if on_pool(t):
                        pool.wait_ge(exp_done, START + TILES * b + t + 1)
                        pool.tensor_tensor(Ps[:, t % TPG, :], Ps[:, t % TPG, :], dec[:, kind_of(t), :],
                                           ALU.mult).then_inc(dec_pool, 1)

            def slot(i, s=None, c=None, e=None, last=False):
                if s is not None:
                    if i == 0 and not first(s):
                        s_values_in(s)
                    decay_tiles(s, i)
                    if i == 4 and not last:
                        s_norm_step(s + 1)
                if c is not None:
                    if i == 2:
                        x_norm_step(c, 0)
                    elif i == 11:
                        x_norm_step(c, 1)
                if s is not None and i == 2:
                    s_bias(s)

            s_norm_step(0)
            s_values_in(0)
            batches(pool, slot)

        @block.scalar
        def _(act):
            act.wait_ge(w_in, 16 * N_W)

            def copy(dst, src, signal):
                act.activation(dst, src, ACT.Copy).then_inc(signal, 1)

            def s_front(b):
                act.wait_ge(s_tr, START + b + 1)
                act.wait_ge(s_proj, START + 3 * b)
                copy(xnT[:, :], mx_bank[0][:, :], mb_free[0])

            def s_queries_keys(b):
                for i, part in ((0, q_part), (1, k_part)):
                    act.wait_ge(s_proj, START + 3 * b + 1 + i)
                    act.wait_ge(scr_out, START + 48 * b)
                    act.wait_ge(s_split, START + 6 * b)
                    ps = mx_bank[1 - i]
                    act.activation(qk_f[:, i, :], ps[:, :], ACT.Identity, bias=bcol[:, i:i + 1])
                    act.activation(part[:, 0, :], ps[:, :], ACT.Identity, bias=bcol[:, i:i + 1])\
                       .then_inc(mb_free[1 - i], 1)

            def s_max_row(b, grp):
                act.wait_ge(mx_tr, START + 4 * b + grp + 1)
                act.wait_ge(max_row, START + 128 * b + 32 * grp)
                copy(mxT[:, :], mx_bank[1][0:NPART * 4, 0:N // 2].bitcast(BF16), mb_free[1])

            def s_exp(b, i, t):
                act.wait_ge(sc_ready, START + TILES * b + t + 1)
                act.wait_ge(pv_done, START + (max(i - 2, 0) if first(b) else SLOTS * b + i - 2))
                act.activation(Ps[:, t % TPG, :], sc_bank[t % 2][:, :], ACT.Exp, scale=SCALE)\
                   .then_inc(exp_done, 1)

            def s_out(b, half):
                act.wait_ge(pv_done, START + SLOTS * b + 6 * half + 6)
                if not first(b):
                    act.wait_ge(c_ready, START + c_written(b - 1, XMAX))
                copy(Nh[:, half, :], s_bank[:, :], sb_free)

            def s_at(b):
                act.wait_ge(c_ready, START + c_written(b, AT))
                copy(atT[:, :], c_bank[AT % 2][:, :], c_free[AT % 2])

            def c_context(b):
                act.wait_ge(c_ready, START + c_written(b, CT))
                copy(cT[:, :], c_bank[CT % 2][:, 0:NK], c_free[CT % 2])

            def c_keys(b):
                act.wait_ge(c_ready, START + c_written(b, KV))
                act.wait_ge(xscr_out, START + 48 * b)
                act.activation(kx_f[:, :], c_bank[KV % 2][:, 0:NK], ACT.Identity, bias=bcol[:, 3:4])
                act.activation(kx_part[:, 0, :], c_bank[KV % 2][:, 0:NK], ACT.Identity, bias=bcol[:, 3:4])\
                   .then_inc(kx_ready, 1)

            def c_norm(b):
                act.wait_ge(c_ready, START + c_written(b, XNT))
                copy(xn2T[:, :], c_bank[XNT % 2][:, :], c_free[XNT % 2])

            def c_queries(b):
                act.wait_ge(c_ready, START + c_written(b, XQ))
                act.activation(qx_f[:, :], c_bank[XQ % 2][:, :], ACT.Identity, bias=bcol[:, 2:3])
                act.activation(qx_part[:, 0, :], c_bank[XQ % 2][:, :], ACT.Identity, bias=bcol[:, 2:3])\
                   .then_inc(c_free[XQ % 2], 1)

            def c_max_row(b):
                act.wait_ge(xb_ready, START + 10 * b + 1)
                act.wait_ge(xmax_row, START + 32 * b)
                copy(mxxT[:, :], x_bank[0:NPART * H, 0:N // 2].bitcast(BF16), xb_free)

            def c_exp(b, t):
                u = XSCORE + t
                act.wait_ge(c_ready, START + c_written(b, u))
                act.wait_ge(xpv_done, START + 4 * b + max(t // 4 - 1, 0))
                act.activation(Px[:, t % 8, :], c_bank[u % 2][:, :], ACT.Exp, scale=SCALE)\
                   .then_inc(c_free[u % 2], 1)

            def c_out(b, half):
                act.wait_ge(xpv_done, START + 4 * b + 2 * half + 2)
                copy(Nx[:, half, :], x_bank[:, :], xb_free)

            def experts_in(b):
                act.wait_ge(xb_ready, START + 10 * b + 4)
                copy(xeT[:, :], x_bank[:, :], xb_free)

            def logits(b):
                act.wait_ge(xb_ready, START + 10 * b + 5)
                act.activation(eg[:, :, :], x_bank[:, 0:NT * E].rearrange("p (t e) -> p t e", e=E),
                               ACT.Exp, scale=-1.0).then_inc(xb_free, 1)

            def expert(b, c):
                act.wait_ge(c_ready, START + e_written(b, c, 0))
                act.activation(th[:, :], c_bank[0][:, :], ACT.Tanh, scale=0.5).then_inc(tanh_done, 1)

            def weights(b):
                act.wait_ge(xb_ready, START + 10 * b + 6)
                copy(combT[0:NPART * E, :], x_bank[0:NPART * E, 0:N // 2].bitcast(BF16), xb_free)

            def slot(i, s=None, c=None, e=None, last=False):
                for j in range(STEPS):
                    at = (i, j)
                    if s is not None:
                        for t in s_tiles(i, j):
                            s_exp(s, i, t)
                        if i % 3 == 2 and j == 0 and not (last and i == 11):
                            s_max_row(s + (i == 11), (i // 3 + 1) % 4)
                        if at == (6, 2):
                            s_out(s, 0)
                        elif not last:
                            if at == (5, 1):
                                s_front(s + 1)
                            elif at == (5, 2):
                                s_queries_keys(s + 1)
                    if c is not None:
                        for t in X_SCORES.get(at, ()):
                            c_exp(c, t)
                        if at == (0, 2):
                            s_out(c, 1)
                            c_context(c)
                        elif at == (0, 3):
                            c_keys(c)
                        elif at == (1, 1):
                            s_at(c)
                        elif at == (2, 3):
                            c_norm(c)
                        elif at == (3, 1):
                            c_queries(c)
                        elif at == (6, 3):
                            c_max_row(c)
                        elif at == (9, 1):
                            c_out(c, 0)
                        elif at == (10, 3):
                            c_out(c, 1)
                    if e is not None:
                        if at == (0, 1):
                            experts_in(e)
                        elif at == (0, 3):
                            logits(e)
                        elif at == (1, 0):
                            expert(e, 0)
                        elif at == (1, 2):
                            weights(e)
                        elif at == (2, 0):
                            expert(e, 1)
                        elif at == (2, 1):
                            expert(e, 2)
                        elif at == (2, 3):
                            expert(e, 3)
                        elif at == (3, 0):
                            expert(e, 4)

            s_front(0)
            s_queries_keys(0)
            s_max_row(0, 0)
            batches(act, slot)

        @block.vector
        def _(dve):
            for stack in (Ks, Qx, Kx):
                dve.memset(stack[ROWX:P, :, :].bitcast(F32), TWO_ONES)
            dve.memset(mask_s[:, 0, :], FAR).then_inc(mask_ready, 1)
            dve.wait_ge(mask_in, 48)
            dve.wait_ge(mask_ready, 1)
            dve.tensor_scalar(mask_s[:, 0, 0:NK], mask_i[:, :], 1.0, 10000.0 / SCALE,
                              ALU.subtract, ALU.mult).then_inc(mask_ready, 1)
            dve.wait_ge(mask_ready, 2)
            dve.tensor_copy(mask_b[:, 0, :], mask_s[:, 0, :]).then_inc(mask_ready, 1)
            dve.wait_ge(mask_ready, 3)
            dve.tensor_tensor(mask_s[:, 1, :], mask_s[:, 0, :], mask_b[:, 0, :], ALU.subtract)\
               .then_inc(mask_ready, 1)
            dve.wait_ge(mask_ready, 4)
            dve.tensor_copy(mask_b[:, 1, :], mask_s[:, 1, :]).then_inc(mask_ready, 1)
            dve.wait_ge(mask_ready, 5)
            dve.tensor_tensor(mask_b[:, 2, :], mask_s[:, 1, :], mask_b[:, 1, :], ALU.subtract)\
               .then_inc(mask_ready, 1)
            dve.wait_ge(w_in, 16 * N_W)
            dve.wait_ge(preset, 3)
            dve.tensor_copy(id_b[:, :], id_f[:, :])
            dve.tensor_copy(diag_b[:, :], diag_f[:, :])
            dve.tensor_copy(sel_b[:, :, :], sel_f[:, :, :]).then_inc(set_up, 1)

            def carry(i):
                dve.memset(spare[0:1, i:i + 1], 0.0)

            def norm_stats(src, st, m, steps, at):
                for t in range(NT):
                    last = dve.bn_stats(st[:, t, :], src[:, t, :])
                last.then_inc(steps, 1)
                dve.wait_ge(steps, START + at + 1)
                carry(0)
                for t in range(NT):
                    last = dve.bn_aggr(m[:, t, :], st[:, t, :])
                last.then_inc(steps, 1)

            def norm_apply(src, m, r, dst, steps, at, scale_sem, scale_at):
                dve.wait_ge(steps, START + at + 2)
                dve.wait_ge(scale_sem, START + scale_at)
                for t in range(NT):
                    last = dve.tensor_scalar(dst[:, t, :], src[:, t, :], m[:, t, 0:1], r[:, t:t + 1],
                                             ALU.subtract, ALU.mult)
                last.then_inc(steps, 1)

            def s_stats(b):
                dve.wait_ge(x_in, START + 16 * b + 16)
                norm_stats(xin, stats, mv, s_ln, 3 * b)

            def s_apply(b):
                dve.wait_ge(s_tr, START + b)
                norm_apply(xin, mv, rstd, xn, s_ln, 3 * b, s_rstd, 2 * b + 2)

            def s_front(b):
                n = front_uses(b)
                dve.wait_ge(scr_out, START + 48 * b)
                for i, part in ((0, q_part), (1, k_part)):
                    dve.wait_ge(mb_free[1 - i], START + n + 1 + i)
                    dve.tensor_tensor(qk_r[:, i, :], qk_f[:, i, :], part[:, 0, :], ALU.subtract)\
                       .then_inc(s_split, 1)
                for i, part in ((0, q_part), (1, k_part)):
                    dve.wait_ge(s_split, START + 6 * b + 1 + i)
                    dve.tensor_copy(part[:, 1, :], qk_r[:, i, :]).then_inc(s_split, 1)
                for i, part in ((0, q_part), (1, k_part)):
                    dve.wait_ge(s_split, START + 6 * b + 3 + i)
                    dve.tensor_tensor(part[:, 2, :], qk_r[:, i, :], part[:, 1, :], ALU.subtract)\
                       .then_inc(s_split, 1)
                dve.wait_ge(s_proj, START + 3 * b + 3)
                dve.wait_ge(v_in, START + b)
                dve.tensor_copy(v_sb[:, :, :], mx_bank[1][:, :].rearrange("p (t d) -> p t d", d=P))\
                   .then_inc(mb_free[1], 1)

            def s_max(b, grp, n, last):
                base = max_uses(b, grp, last)
                qt, g, k = MAX_TILES[n]
                dve.wait_ge(max_ready, START + 4 * NM * b + NM * grp + n + 1)
                if n == 0:
                    dve.wait_ge(mx_split, START + 16 * b + 4 * grp)
                w = P * (qt + 1)
                dve.tensor_reduce(mx[:, qt, g:g + k],
                                  mx_bank[n % 2][:, 0:k * w].rearrange("p (h k) -> p h k", k=w),
                                  axis=AX_X, op=ALU.max, negate=True).then_inc(mb_free[n % 2], 1)
                if n == NM - 1:
                    dve.wait_ge(mb_free[0], START + base + (NM + 1) // 2)
                    dve.wait_ge(mb_free[1], START + base + NM // 2)
                    dve.wait_ge(mx_tr, START + 4 * b + grp)
                    split(mx, mx_r, mx_part, mx_split, 16 * b + 4 * grp)

            def split(src, rest, part, steps, at):
                dve.tensor_copy(part[:, :, 0, :], src[:, :, :]).then_inc(steps, 1)
                dve.wait_ge(steps, START + at + 1)
                dve.tensor_tensor(rest[:, :, :], src[:, :, :], part[:, :, 0, :], ALU.subtract).then_inc(steps, 1)
                dve.wait_ge(steps, START + at + 2)
                dve.tensor_copy(part[:, :, 1, :], rest[:, :, :]).then_inc(steps, 1)
                dve.wait_ge(steps, START + at + 3)
                dve.tensor_tensor(part[:, :, 2, :], rest[:, :, :], part[:, :, 1, :], ALU.subtract)\
                   .then_inc(steps, 1)

            def s_decay(b, t):
                if not on_pool(t):
                    dve.wait_ge(exp_done, START + TILES * b + t + 1)
                    dve.tensor_tensor(Ps[:, t % TPG, :], Ps[:, t % TPG, :], dec[:, kind_of(t), :],
                                      ALU.mult).then_inc(dec_dve, 1)

            def normalise(b, half, ps, d, dst, ready, ready_at, steps, steps_at, free):
                v = ps[:, :].rearrange("p (u c) -> p u c", c=32)
                dve.wait_ge(ready, START + ready_at)
                dve.wait_ge(steps, START + steps_at)
                dve.reciprocal(d[:, :, :], v[:, :, 16:32:8]).then_inc(steps, 1)
                dve.wait_ge(steps, START + steps_at + 1)
                for e in range(2):
                    to = dst[:, :, 64 * half:64 * half + 64].rearrange("p t (g c) -> p t g c", g=4)
                    last = dve.tensor_tensor(to[:, :, :, DK * e:DK * e + DK],
                                             v[:, :, DK * e:DK * e + DK].rearrange("p (t g) d -> p t g d", g=4),
                                             d[:, :, e:e + 1].rearrange("p (t g) o -> p t g o", g=4)
                                             .broadcast_to([P, NT, 4, DK]), ALU.mult)
                last.then_inc(free, 1)

            def s_tail(b, half):
                u = HALF[half]
                if half:
                    dve.wait_ge(c_free[HALF[0] % 2], START + c_uses(b, HALF[0]) + 1)
                normalise(b, half, c_bank[u % 2], den, at, c_ready, c_written(b, u), s_norm, 2 * b + half,
                          c_free[u % 2])

            def s_result(b):
                dve.wait_ge(c_ready, START + c_written(b, OUT_PROJ))
                dve.wait_ge(xb_done, START + b + 1)
                dve.wait_ge(x_norm, START + 3 * b)
                dve.tensor_tensor(x1[:, :, :], c_bank[OUT_PROJ % 2][:, :].rearrange("p (t d) -> p t d", d=P),
                                  xb[:, :, :], ALU.add).then_inc(c_free[OUT_PROJ % 2], 1)

            def c_keys(b):
                dve.wait_ge(kx_ready, START + b + 1)
                dve.wait_ge(xpv_done, START + 4 * b)
                for e in range(2):
                    src = c_bank[KV % 2][0:NK, P:2 * P].rearrange("p (g e d) -> p g e d", e=2, d=DK)[:, :, e, :]
                    bv = brow[0:NK, 2, :].rearrange("p (g e d) -> p g e d", e=2, d=DK)[:, :, e, :]
                    last = dve.tensor_tensor(Vx[0:NK, e:H:2, DK * e:DK * e + DK], src, bv, ALU.add)
                last.then_inc(c_free[KV % 2], 1)
                dve.tensor_tensor(kx_r[:, :], kx_f[:, :], kx_part[:, 0, :], ALU.subtract).then_inc(x_split, 1)
                dve.wait_ge(x_split, START + 6 * b + 1)
                dve.tensor_copy(kx_part[:, 1, :], kx_r[:, :]).then_inc(x_split, 1)
                dve.wait_ge(x_split, START + 6 * b + 2)
                dve.tensor_tensor(kx_part[:, 2, :], kx_r[:, :], kx_part[:, 1, :], ALU.subtract)\
                   .then_inc(x_split, 1)

            def c_stats(b):
                dve.wait_ge(c_free[OUT_PROJ % 2], START + c_uses(b, OUT_PROJ) + 1)
                norm_stats(x1, statsx, mvx, x_ln, 6 * b)

            def c_apply(b):
                norm_apply(x1, mvx, rstdx, xn2, x_ln, 6 * b, x_rstd, 4 * b + 2)

            def c_front(b):
                dve.wait_ge(c_free[XQ % 2], START + c_uses(b, XQ) + 1)
                dve.tensor_tensor(qx_r[:, :], qx_f[:, :], qx_part[:, 0, :], ALU.subtract).then_inc(x_split, 1)
                dve.wait_ge(x_split, START + 6 * b + 4)
                dve.tensor_copy(qx_part[:, 1, :], qx_r[:, :]).then_inc(x_split, 1)
                dve.wait_ge(x_split, START + 6 * b + 5)
                dve.tensor_tensor(qx_part[:, 2, :], qx_r[:, :], qx_part[:, 1, :], ALU.subtract)\
                   .then_inc(x_split, 1)

            def c_max(b, n):
                qt, h, k = XMAX_TILES[n]
                u = XMAX + n
                dve.wait_ge(c_ready, START + c_written(b, u))
                dve.tensor_reduce(mxx[:, qt, h:h + k],
                                  c_bank[u % 2][:, 0:k * NK].rearrange("p (h k) -> p h k", k=NK),
                                  axis=AX_X, op=ALU.max, negate=True).then_inc(c_free[u % 2], 1)

            def c_max_split(b):
                for k in range(2):
                    dve.wait_ge(c_free[k], START + c_uses(b, XSCORE))
                split(mxx, mxx_r, mxx_part, xmx_split, 4 * b)

            def c_tail(b, half):
                if half:
                    dve.wait_ge(xb_free, START + 8 * b + 4)
                normalise(b, half, x_bank, denx, atx, xb_ready, 10 * b + 2 + half, x_norm,
                          3 * b + half, xb_free)

            def c_result(b):
                dve.wait_ge(xb_free, START + 8 * b + 5)
                dve.wait_ge(y_ready, START + b)
                dve.tensor_tensor(x2[:, :, :], x1[:, :, :], atx[:, :, :], ALU.add).then_inc(x_norm, 1)
                dve.wait_ge(x_norm, START + 3 * b + 3)
                norm_stats(x2, statsx, mvx, x_ln, 6 * b + 3)

            def routing(b):
                at = 12 * b
                dve.wait_ge(xb_free, START + 8 * b + 7)
                dve.tensor_scalar(sg[:, :, :], eg[:, :, :], 1.0, None, ALU.add).then_inc(g_step, 1)
                dve.wait_ge(g_step, START + at + 1)
                dve.reciprocal(eg[:, :, :], sg[:, :, :]).then_inc(g_step, 1)
                dve.wait_ge(g_step, START + at + 2)
                carry(1)
                for t in range(NT):
                    last = dve.max(top[:, t, :], eg[:, t, :])
                last.then_inc(g_step, 1)
                dve.wait_ge(g_step, START + at + 3)
                carry(2)
                for t in range(NT):
                    last = dve.max_index(topi[:, t, :], top[:, t, :], eg[:, t, :])
                dve.scalar_tensor_tensor(wsum[:, :, :], top[:, :, 0:1], 1e-20, top[:, :, 1:2], ALU.add, ALU.add)\
                   .then_inc(g_step, 1)
                dve.wait_ge(g_step, START + at + 4)
                dve.tensor_copy(topf[:, :, :], topi[:, :, 0:2])
                dve.reciprocal(wsum[:, :, :], wsum[:, :, :]).then_inc(g_step, 1)
                dve.wait_ge(g_step, START + at + 5)
                dve.scalar_tensor_tensor(topw[:, :, :], top[:, :, 0:2], ROUTE, wsum[:, :, :].broadcast_to([P, NT, 2]),
                                         ALU.mult, ALU.mult).then_inc(g_step, 1)
                dve.wait_ge(g_step, START + at + 6)
                for k in range(2):
                    for t in range(NT):
                        last = dve.tensor_scalar(comb[:, k, t, :], iota_sb[:, :], topf[:, t, k:k + 1],
                                                 topw[:, t, k:k + 1], ALU.is_equal, ALU.mult)
                last.then_inc(g_step, 1)
                dve.wait_ge(g_step, START + at + 7)
                dve.tensor_tensor(comb_f[:, :, :], comb[:, 0], comb[:, 1], ALU.add).then_inc(g_step, 1)
                dve.wait_ge(g_step, START + at + 8)
                split(comb_f, comb_r, comb_part, g_step, at + 8)

            def expert(b, c):
                dve.wait_ge(tanh_done, START + FC * b + c + 1)
                dve.scalar_tensor_tensor(ga[:, :], th[:, :], 1.0, c_bank[0][:, :],
                                         ALU.add, ALU.mult).then_inc(c_free[0], 1)
                dve.wait_ge(c_ready, START + e_written(b, c, 1))
                dve.wait_ge(c_free[0], START + e_uses(b, c, 0) + 1)
                dve.scalar_tensor_tensor(hm[:, c, :], ga[:, :], 0.5, c_bank[1][:, :],
                                         ALU.mult, ALU.mult).then_inc(c_free[1], 1)

            def expert_weight(b, c):
                if c < FC - 1:
                    dve.wait_ge(xb_ready, START + 10 * b + 7 + c)
                    dve.wait_ge(c_free[1], START + e_uses(b, c, 1) + 1)
                    dve.tensor_tensor(hm[:, c, :], hm[:, c, :], x_bank[:, :], ALU.mult)\
                       .then_inc(gate_done, 1)

            def result(b):
                dve.wait_ge(down_done, START + b + 1)
                dve.wait_ge(y_out, START + 16 * b)
                dve.tensor_tensor(yo[:, :, :], x_bank[:, :].rearrange("p (t d) -> p t d", d=P), x2[:, :, :],
                                  ALU.add).then_inc(y_ready, 1)

            def slot(i, s=None, c=None, e=None, last=False):
                for j in range(STEPS):
                    at = (i, j)
                    if s is not None:
                        if max_stage(i, last):
                            for n in maxima(i, j):
                                s_max(*max_group(s, i), n, last)
                        if j:
                            for t in s_tiles(i, j - 1):
                                s_decay(s, t)
                        if j == STEPS - 1:
                            for t in s_tiles(i, j):
                                s_decay(s, t)
                        if not last:
                            if at == (4, 3):
                                s_stats(s + 1)
                            elif at == (5, 0):
                                s_apply(s + 1)
                            elif at == (5, 2):
                                s_front(s + 1)
                    if c is not None:
                        for n in X_MAX.get(at, ()):
                            c_max(c, n)
                        if at == (0, 1):
                            s_tail(c, 0)
                        elif at == (0, 3):
                            c_keys(c)
                        elif at == (1, 0):
                            s_tail(c, 1)
                        elif at == (2, 0):
                            s_result(c)
                            c_stats(c)
                        elif at == (2, 2):
                            c_apply(c)
                        elif at == (3, 2):
                            c_front(c)
                        elif at == (6, 1):
                            c_max_split(c)
                        elif at == (11, 0):
                            c_tail(c, 0)
                        elif at == (11, 2):
                            c_tail(c, 1)
                            c_result(c)
                    if e is not None:
                        if at == (0, 0):
                            norm_apply(x2, mvx, rstdx, xe, x_ln, 6 * e + 3, x_rstd, 4 * e + 4)
                        elif at == (0, 3):
                            routing(e)
                        elif at == (1, 1):
                            expert(e, 0)
                        elif at == (1, 3):
                            expert_weight(e, 0)
                        elif at == (2, 1):
                            expert(e, 1)
                            expert_weight(e, 1)
                        elif at == (2, 2):
                            expert(e, 2)
                            expert_weight(e, 2)
                        elif at == (3, 0):
                            expert(e, 3)
                            expert_weight(e, 3)
                        elif at == (3, 1):
                            expert(e, 4)
                        elif at == (3, 3):
                            result(e)

            s_stats(0)
            s_apply(0)
            s_front(0)
            for n in range(NM):
                s_max(0, 0, n, False)
            for n in range(3):
                s_max(0, 1, n, False)
            batches(dve, slot)

        @block.tensor
        def _(pe):
            def mm(dst, lhsT, rhs, start=True, stop=True):
                return pe.matmul(dst, lhsT, rhs, start=start, stop=stop, skip_group_check=True)

            def s_front(b):
                n = front_uses(b)
                pe.wait_ge(s_ln, START + 3 * b + 3)
                pe.wait_ge(mb_free[0], START + n)
                for t in range(NT):
                    last = pe.transpose(mx_bank[0][:, P * t:P * t + P], xn[:, t, :], id_f[:, :])
                last.then_inc(s_tr, 1)

            def s_project(b):
                n = front_uses(b)
                pe.wait_ge(mb_free[0], START + n + 1)
                pe.wait_ge(mb_free[1], START + n)
                mm(mx_bank[1][:, :], w_sb[:, WQ, :], xnT[:, :]).then_inc(s_proj, 1)
                mm(mx_bank[0][:, :], w_sb[:, WK, :], xnT[:, :]).then_inc(s_proj, 1)
                pe.wait_ge(mb_free[1], START + n + 1)
                for t in range(NT):
                    last = mm(mx_bank[1][:, P * t:P * t + P], xnT[:, P * t:P * t + P], w_sb[:, WV, :])
                last.then_inc(s_proj, 1)

            def s_max(b, grp, n, last):
                half, e = GROUPS[grp]
                qt, g0, k = MAX_TILES[n]
                w = P * (qt + 1)
                if n == 0:
                    pe.wait_ge(stack_in[half], START + 96 * b + 96)
                pe.wait_ge(mb_free[n % 2], START + max_uses(b, grp, last) + n // 2)
                for i in range(k):
                    h = head(half, e, g0 + i)
                    mm(mx_bank[n % 2][:, w * i:w * i + w], Qs[0:KM, h, P * qt:P * qt + P],
                       Ks[0:KM, h, 0:w], stop=False)
                    ins = mm(mx_bank[n % 2][:, w * i + w - P:w * i + w], id_b[:, :], diag_b[:, :],
                             start=False)
                ins.then_inc(max_ready, 1)

            def s_max_turn(b, grp, last):
                pe.wait_ge(mx_split, START + 16 * b + 4 * grp + 4)
                pe.wait_ge(mb_free[1], START + max_uses(b, grp, last) + NM // 2)
                for t in range(NT):
                    ins = pe.transpose(mx_bank[1][:, P // 2 * t:P // 2 * (t + 1)].bitcast(BF16),
                                       mx_part[:, t].rearrange("p i h -> p (i h)"), id_b[:, :])
                ins.then_inc(mx_tr, 1)

            def s_scores(b, t):
                half, e = GROUPS[t // TPG]
                if t % TPG == 0:
                    pe.wait_ge(max_row, START + 128 * b + 32 * (t // TPG) + 32)
                if t >= 2:
                    pe.wait_ge(exp_done, START + TILES * b + t - 1)
                else:
                    pe.wait_ge(exp_done, START + TILES * b)
                for g, kt, c in PIECES[t % TPG]:
                    h = head(half, e, g)
                    w = N - P * kt
                    last = mm(sc_bank[t % 2][:, c:c + w], Ks[0:KS, h, P * kt:P * kt + P],
                              Qs[0:KS, h, P * kt:N])
                last.then_inc(sc_ready, 1)

            def s_values(b, s):
                half, e = GROUPS[s // 3]
                if s % 6 == 0:
                    pe.wait_ge(v_in, START + b + 1)
                    pe.wait_ge(sb_free, START + 2 * b + s // 6)
                t1 = TPG * (s // 3) + SETS[s % 3][1] - 1
                pe.wait_ge(dec_dve, START + DVE_N * b + applied_before(t1, False))
                pe.wait_ge(dec_pool, START + POOL_N * b + applied_before(t1, True))
                pieces = [(i, *piece) for i in range(*SETS[s % 3]) for piece in PIECES[i]]
                for i, g, kt, c in sorted(pieces, key=lambda p: (p[2], p[1])):
                    h = head(half, e, g)
                    w = N - P * kt
                    last = mm(s_bank[32 * g:32 * g + 32, P * kt:N], Vs[:, kt, h, :], Ps[:, i, c:c + w],
                              start=(e == 0 and kt == 0), stop=(e == 1 and kt == 2))
                last.then_inc(pv_done, 1)

            def c_use(b, u):
                pe.wait_ge(c_free[u % 2], START + c_uses(b, u))
                return c_bank[u % 2]

            def s_tail(b, half):
                pe.wait_ge(sb_free, START + 2 * b + 1 + half)
                ps = c_use(b, HALF[half])
                for t in range(NT):
                    last = pe.transpose(ps[:, P * t:P * t + P], Nh[:, half, P * t:P * t + P], id_f[:, :])
                last.then_inc(c_ready, 1)

            def s_at(b):
                pe.wait_ge(c_free[HALF[1] % 2], START + c_uses(b, HALF[1]) + 1)
                ps = c_use(b, AT)
                for t in range(NT):
                    last = pe.transpose(ps[:, P * t:P * t + P], at[:, t, :], id_f[:, :])
                last.then_inc(c_ready, 1)

            def s_out_proj(b):
                pe.wait_ge(c_free[AT % 2], START + c_uses(b, AT) + 1)
                ps = c_use(b, OUT_PROJ)
                for t in range(NT):
                    last = mm(ps[:, P * t:P * t + P], atT[:, P * t:P * t + P], w_sb[:, WO, :])
                last.then_inc(c_ready, 1)

            def c_context(b):
                ps = c_use(b, CT)
                pe.wait_ge(ctx_in_s, START + 16 * b + 16)
                pe.transpose(ps[:, 0:NK], cin[:, :], id_f[0:NK, 0:NK]).then_inc(c_ready, 1)

            def c_keys(b):
                pe.wait_ge(c_free[CT % 2], START + c_uses(b, CT) + 1)
                ps = c_use(b, KV)
                mm(ps[:, 0:NK], w_sb[:, WXK, :], cT[:, :])
                mm(ps[0:NK, P:2 * P], cT[:, :], w_sb[:, WXV, :]).then_inc(c_ready, 1)

            def c_norm(b):
                pe.wait_ge(x_ln, START + 6 * b + 3)
                ps = c_use(b, XNT)
                for t in range(NT):
                    last = pe.transpose(ps[:, P * t:P * t + P], xn2[:, t, :], id_f[:, :])
                last.then_inc(c_ready, 1)

            def c_queries(b):
                pe.wait_ge(c_free[XNT % 2], START + c_uses(b, XNT) + 1)
                ps = c_use(b, XQ)
                mm(ps[:, :], w_sb[:, WXQ, :], xn2T[:, :]).then_inc(c_ready, 1)

            def c_max(b, n):
                if n == 0:
                    pe.wait_ge(xk_in, START + 48 * b + 48)
                    pe.wait_ge(mask_rows, START + 48 * b + 48)
                    pe.wait_ge(xq_in, START + 48 * b + 48)
                qt, h0, k = XMAX_TILES[n]
                ps = c_use(b, XMAX + n)
                for i in range(k):
                    last = mm(ps[:, NK * i:NK * i + NK], Qx[0:KMX, h0 + i, P * qt:P * qt + P],
                              Kx[0:KMX, h0 + i, 0:NK])
                last.then_inc(c_ready, 1)

            def c_max_turn(b):
                pe.wait_ge(xmx_split, START + 4 * b + 4)
                pe.wait_ge(y_ready, START + b)
                for t in range(NT):
                    last = pe.transpose(x_bank[:, P // 2 * t:P // 2 * (t + 1)].bitcast(BF16),
                                        mxx_part[:, t].rearrange("p i h -> p (i h)"), id_b[:, :])
                last.then_inc(xb_ready, 1)

            def c_score(b, t):
                if t == 0:
                    pe.wait_ge(xmax_row, START + 32 * b + 32)
                h = head(t // 8, t // 4 % 2, t % 4)
                ps = c_use(b, XSCORE + t)
                mm(ps[:, :], Kx[0:KSX, h, :], Qx[0:KSX, h, :]).then_inc(c_ready, 1)

            def c_values(b, v):
                for k in range(2):
                    pe.wait_ge(c_free[k], START + c_uses(b, XSCORE + 4 * v) + 2)
                if v % 2 == 0:
                    pe.wait_ge(xb_free, START + 8 * b + 1 + v // 2)
                for g in range(4):
                    last = mm(x_bank[32 * g:32 * g + 32, :], Vx[:, head(v // 2, v % 2, g), :],
                              Px[:, 4 * (v % 2) + g, :], start=v % 2 == 0, stop=v % 2 == 1)
                last.then_inc(xpv_done, 1)

            def c_tail(b, half):
                pe.wait_ge(xb_free, START + 8 * b + 3 + half)
                for t in range(NT):
                    last = pe.transpose(x_bank[:, P * t:P * t + P], Nx[:, half, P * t:P * t + P], id_f[:, :])
                last.then_inc(xb_ready, 1)

            def experts_in(b):
                pe.wait_ge(x_ln, START + 6 * b + 6)
                pe.wait_ge(xb_free, START + 8 * b + 5)
                for t in range(NT):
                    last = pe.transpose(x_bank[:, P * t:P * t + P], xe[:, t, :], id_f[:, :])
                last.then_inc(xb_ready, 1)

            def logits(b):
                pe.wait_ge(xb_free, START + 8 * b + 6)
                for t in range(NT):
                    last = mm(x_bank[:, E * t:E * t + E], xeT[:, P * t:P * t + P], gate_sb[:, :])
                last.then_inc(xb_ready, 1)

            def expert(b, c):
                for k, w in enumerate((wg_sb, wu_sb)):
                    pe.wait_ge(c_free[k], START + e_uses(b, c, k))
                    mm(c_bank[k][:, :], w[:, P * c:P * c + P], xeT[:, :]).then_inc(c_ready, 1)

            def weights(b):
                pe.wait_ge(g_step, START + 12 * b + 12)
                pe.wait_ge(xb_free, START + 8 * b + 7)
                for t in range(NT):
                    last = pe.transpose(x_bank[:, P // 2 * t:P // 2 * (t + 1)].bitcast(BF16),
                                        comb_part[:, t].rearrange("p i e -> p (i e)"), id_b[:, :])
                last.then_inc(xb_ready, 1)

            def expert_weight(b, c):
                if c:
                    pe.wait_ge(gate_done, START + 4 * b + c)
                else:
                    pe.wait_ge(xb_free, START + 8 * b + 8)
                mm(x_bank[:, :], sel_b[:, c, :], combT[:, :]).then_inc(xb_ready, 1)

            def experts_out(b):
                pe.wait_ge(gate_done, START + 4 * b + 4)
                pe.wait_ge(c_free[1], START + e_uses(b, FC - 1, 1) + 1)
                for t in range(NT):
                    for c in range(FC):
                        last = mm(x_bank[:, P * t:P * t + P], hm[:, c, P * t:P * t + P], wd_sb[:, c, :],
                                  start=c == 0, stop=c == FC - 1)
                last.then_inc(down_done, 1)

            pe.wait_ge(w_in, 16 * N_W)
            pe.wait_ge(mask_in, 48)
            pe.wait_ge(preset, 3)
            pe.wait_ge(set_up, 1)

            def slot(i, s=None, c=None, e=None, last=False):
                for j in range(STEPS):
                    at = (i, j)
                    if s is not None:
                        for t in s_tiles(i, j):
                            s_scores(s, t)
                        if i and j == (1 if i % 3 < 2 else 0):
                            s_values(s, i - 1)
                        if i % 3 == 2 and j == 0 and not (last and i == 11):
                            s_max_turn(s + (i == 11), (i // 3 + 1) % 4, last)
                        if not last:
                            if at == (5, 1):
                                s_front(s + 1)
                            elif at == (5, 2):
                                s_project(s + 1)
                        if max_stage(i, last):
                            for n in maxima(i, j):
                                s_max(*max_group(s, i), n, last)
                    if c is not None:
                        for n in X_MAX.get(at, ()):
                            c_max(c, n)
                        if at in X_VALUES:
                            c_values(c, X_VALUES[at])
                        for t in X_SCORES.get(at, ()):
                            c_score(c, t)
                        if at == (0, 0):
                            s_tail(c, 0)
                        elif at == (0, 1):
                            s_values(c, SLOTS - 1)
                            c_context(c)
                        elif at == (0, 2):
                            c_keys(c)
                        elif at == (0, 3):
                            s_tail(c, 1)
                        elif at == (1, 1):
                            s_at(c)
                        elif at == (1, 3):
                            s_out_proj(c)
                        elif at == (2, 3):
                            c_norm(c)
                        elif at == (3, 1):
                            c_queries(c)
                        elif at == (6, 3):
                            c_max_turn(c)
                        elif at == (11, 0):
                            c_tail(c, 0)
                        elif at == (11, 2):
                            c_tail(c, 1)
                    if e is not None:
                        if at == (0, 0):
                            experts_in(e)
                        elif at == (0, 2):
                            logits(e)
                        elif at == (1, 0):
                            expert(e, 0)
                        elif at == (1, 2):
                            weights(e)
                        elif at == (1, 3):
                            expert_weight(e, 0)
                        elif at == (2, 0):
                            expert(e, 1)
                            expert_weight(e, 1)
                        elif at == (2, 1):
                            expert(e, 2)
                            expert_weight(e, 2)
                        elif at == (2, 3):
                            expert(e, 3)
                            expert_weight(e, 3)
                        elif at == (3, 0):
                            expert(e, 4)
                        elif at == (3, 2):
                            experts_out(e)

            s_front(0)
            s_project(0)
            for n in range(NM):
                s_max(0, 0, n, False)
            s_max_turn(0, 0, False)
            for n in range(3):
                s_max(0, 1, n, False)
            batches(pe, slot)


def kernel(**inputs):
    import numpy as np
    import concourse.bacc as bacc
    from concourse.bass_utils import run_bass_kernel_spmd as run

    a = {k: np.ascontiguousarray(v) for k, v in inputs.items()}
    i, j = np.arange(P)[:, None], np.arange(P)[None, :]
    delta = np.arange(N)[None, :] - np.arange(P)[:, None]
    part_expert = np.arange(P)[:, None, None]
    column_expert = 2 * np.arange(4)[None, :, None] + np.arange(P)[None, None, :] // 64
    ffn = "L0_ffn_"

    def by_dim(w):
        return w.reshape(*w.shape[:-1], H, DK).swapaxes(-1, -2).reshape(w.shape)

    arrays = {
        "x": a["x"], "ctx_in": a["ctx_1024"], "mask": a["mask_BxS2_ik0"],
        "wq": by_dim(a["L0_attn_Wq"]), "wk": by_dim(a["L0_attn_Wk"]), "wv": a["L0_attn_Wv"], "wo": a["L0_attn_Wo"],
        "wxq": by_dim(a["L0_xattn_Wq"].T), "wxk": by_dim(a["L0_xattn_Wk"].T), "wxv": a["L0_xattn_Wv"].T,
        "bias_cols": by_dim(np.stack([a["L0_attn_bq"], a["L0_attn_bk"], a["L0_xattn_bq"], a["L0_xattn_bk"]])),
        "bias_rows": np.stack([a["L0_attn_bv"], a["L0_attn_bo"], a["L0_xattn_bv"]]),
        "wg": np.concatenate([a[ffn + "w_gate"].reshape(512, P), a[ffn + "ws_gate"]]).T,
        "wu": np.concatenate([a[ffn + "w_up"].reshape(512, P), a[ffn + "ws_up"]]).T,
        "wd": np.concatenate([a[ffn + "w_down"].transpose(0, 2, 1).reshape(4, P, P), a[ffn + "ws_down"].T[None]]),
        "gate": a[ffn + "gate_weight"].T,
        "ident": np.eye(P, dtype=np.float32),
        "diag": np.where(j > i, np.float32(FAR), np.float32(0)).astype(np.float32),
        "decay": np.where(delta < 0, 0.0, np.maximum(delta, 1).astype(np.float64) ** -0.25).astype(np.float32),
        "sel": np.where(part_expert < NPART * E, part_expert % E == column_expert, False).astype(np.float32),
        "iota": np.tile(np.arange(E, dtype=np.float32), (P, 1)),
    }
    arrays = {k: np.ascontiguousarray(v) for k, v in arrays.items()}
    nc = bacc.Bacc("TRN2", target_bir_lowering=False, num_devices=1)
    args = {k: nc.dram_tensor(k, v.shape, mybir.dt.from_np(v.dtype), kind="ExternalInput").ap()
            for k, v in arrays.items()}
    out = nc.dram_tensor("out", (B, N, P), F32, kind="ExternalOutput").ap()
    decoder_layer(nc, out=out, **args)
    return run(nc, [arrays], core_ids=[0]).results[0]["out"]
```
